# Optimizing a Trainium2 kernel written in Bass

```python
import numpy as np
import jax
import jax.numpy as jnp

def _softmax(x, axis=-1):
    return jax.nn.softmax(x, axis=axis)

def _gelu(x):
    return jax.nn.gelu(x, approximate=True)

def _silu(x):
    return jax.nn.silu(x)

def _sigmoid(x):
    return jax.nn.sigmoid(x)

def _layernorm(x, axis=-1, eps=1e-05):
    m = jnp.mean(x, axis=axis, keepdims=True)
    v = jnp.var(x, axis=axis, keepdims=True)
    return (x - m) / jnp.sqrt(v + eps)

def _scatter_add(tgt, idx, src, axis=0):
    return tgt.at[idx].add(src)

def _segment_sum(src, seg, n):
    return jax.ops.segment_sum(src, seg, n)
kernel_name = 'mk_seq_postln_d1_jaxref_r4_c9b5e2'

def setup_inputs(seed: int=0):
    np.random.seed(seed)
    _w = jnp.asarray

    def _L0_attn_setup():
        import jax, jax.numpy as jnp
        import numpy as np
        B, S, D, H, F = (4, 2048, 256, 16, 64)
        DK = D // H
        EPS = 1e-06

        def _heads(x, W, b):
            y = jnp.einsum('bsd,de->bse', x, W) + b
            return y.reshape(x.shape[0], x.shape[1], H, DK).transpose(0, 2, 1, 3)
        key = jax.random.key(seed)
        ks = jax.random.split(key, 6)
        scale = 1.0 / np.sqrt(D)
        x = jax.random.normal(ks[0], (B, S, D), dtype=jnp.float32)
        Wq = jax.random.normal(ks[1], (D, D), dtype=jnp.float32) * scale
        Wk = jax.random.normal(ks[2], (D, D), dtype=jnp.float32) * scale
        Wv = jax.random.normal(ks[3], (D, D), dtype=jnp.float32) * scale
        Wo = jax.random.normal(ks[4], (D, D), dtype=jnp.float32) * scale
        rw = jax.random.normal(ks[5], (H, DK, F), dtype=jnp.float32) / np.sqrt(DK)
        zb = jnp.zeros((D,), dtype=jnp.float32)
        return {'x': x, 'Wq': Wq, 'bq': zb, 'Wk': Wk, 'bk': zb, 'Wv': Wv, 'bv': zb, 'Wo': Wo, 'bo': zb, 'rw': rw}
    _L0_attn_in = _L0_attn_setup()

    def _L0_ffn_setup():
        import jax, jax.numpy as jnp
        import numpy as np
        B, T, D = (2, 512, 256)
        DCD = 1024
        RET = 128
        NEXP = 1024
        NKEYS = 64
        H = 4
        KPH = 8
        key = jax.random.key(seed)
        ks = jax.random.split(key, 10)
        s = lambda k, shape, scale: jax.random.normal(k, shape, jnp.float32) * scale
        return {'hidden_states': jax.random.normal(ks[0], (B, T, D), jnp.float32), 'Wg': s(ks[1], (D, DCD), 0.02), 'bg': jnp.zeros((DCD,), jnp.float32), 'Wu': s(ks[2], (D, DCD), 0.02), 'bu': jnp.zeros((DCD,), jnp.float32), 'Wd': s(ks[3], (DCD, D), 0.02), 'bd': jnp.zeros((D,), jnp.float32), 'Wq': s(ks[4], (D, RET * H), 0.02), 'keys': s(ks[5], (H, NKEYS, 2, RET // 2), 0.02), 'down_embed': s(ks[6], (NEXP, D), 0.02), 'up_embed': s(ks[7], (NEXP, D), 0.02)}
    _L0_ffn_in = _L0_ffn_setup()
    _d = {'L0_attn_x': _L0_attn_in['x'], 'L0_attn_Wq': _L0_attn_in['Wq'], 'L0_attn_bq': _L0_attn_in['bq'], 'L0_attn_Wk': _L0_attn_in['Wk'], 'L0_attn_bk': _L0_attn_in['bk'], 'L0_attn_Wv': _L0_attn_in['Wv'], 'L0_attn_bv': _L0_attn_in['bv'], 'L0_attn_Wo': _L0_attn_in['Wo'], 'L0_attn_bo': _L0_attn_in['bo'], 'L0_attn_rw': _L0_attn_in['rw'], 'L0_ffn_Wg': _L0_ffn_in['Wg'], 'L0_ffn_bg': _L0_ffn_in['bg'], 'L0_ffn_Wu': _L0_ffn_in['Wu'], 'L0_ffn_bu': _L0_ffn_in['bu'], 'L0_ffn_Wd': _L0_ffn_in['Wd'], 'L0_ffn_bd': _L0_ffn_in['bd'], 'L0_ffn_Wq': _L0_ffn_in['Wq'], 'L0_ffn_keys': _L0_ffn_in['keys'], 'L0_ffn_down_embed': _L0_ffn_in['down_embed'], 'L0_ffn_up_embed': _L0_ffn_in['up_embed']}
    _x0 = _d['L0_attn_x']
    _d['L0_attn_x'] = jax.random.normal(jax.random.fold_in(jax.random.key(seed), 1), (8, 2048, 256), dtype=_x0.dtype)
    del _x0
    return _d

def reference(L0_attn_x, L0_attn_Wq, L0_attn_bq, L0_attn_Wk, L0_attn_bk, L0_attn_Wv, L0_attn_bv, L0_attn_Wo, L0_attn_bo, L0_attn_rw, L0_ffn_Wg, L0_ffn_bg, L0_ffn_Wu, L0_ffn_bu, L0_ffn_Wd, L0_ffn_bd, L0_ffn_Wq, L0_ffn_keys, L0_ffn_down_embed, L0_ffn_up_embed):

    def _L0_attn_ref(x, Wq, bq, Wk, bk, Wv, bv, Wo, bo, rw):
        import jax, jax.numpy as jnp
        import numpy as np
        B, S, D, H, F = (4, 2048, 256, 16, 64)
        DK = D // H
        EPS = 1e-06

        def _heads(x, W, b):
            y = jnp.einsum('bsd,de->bse', x, W) + b
            return y.reshape(x.shape[0], x.shape[1], H, DK).transpose(0, 2, 1, 3)
        q = _heads(x, Wq, bq)
        k = _heads(x, Wk, bk)
        v = _heads(x, Wv, bv)
        qp = jax.nn.relu(jnp.einsum('bhsd,hdf->bhsf', q, rw)) + EPS
        kp = jax.nn.relu(jnp.einsum('bhsd,hdf->bhsf', k, rw)) + EPS
        kv = jnp.einsum('bhsf,bhsd->bhfd', kp, v)
        qkv = jnp.einsum('bhsf,bhfd->bhsd', qp, kv)
        norm = jnp.einsum('bhsf,bhf->bhs', qp, kp.sum(axis=2))
        out = qkv / (norm[..., None] + EPS)
        out = out.transpose(0, 2, 1, 3).reshape(x.shape[0], x.shape[1], D)
        return jnp.einsum('bsd,de->bse', out, Wo) + bo

    def _L0_ffn_ref(hidden_states, Wg, bg, Wu, bu, Wd, bd, Wq, keys, down_embed, up_embed):
        import jax, jax.numpy as jnp
        import numpy as np
        B, T, D = (2, 512, 256)
        DCD = 1024
        RET = 128
        NEXP = 1024
        NKEYS = 64
        H = 4
        KPH = 8
        b, t, d = hidden_states.shape
        q = (hidden_states @ Wq).reshape(b, t, 2, H, RET // 2)
        sim = jnp.einsum('btphn,hkpn->pbthk', q, keys)
        sc, ix = jax.lax.top_k(sim, KPH)
        sx, sy = (sc[0], sc[1])
        ixx, ixy = (ix[0], ix[1])
        all_sc = (sx[..., :, None] + sy[..., None, :]).reshape(b, t, H, KPH * KPH)
        all_ix = (ixx[..., :, None] * NKEYS + ixy[..., None, :]).reshape(b, t, H, KPH * KPH)
        scores, pk = jax.lax.top_k(all_sc, KPH)
        idx = jnp.take_along_axis(all_ix, pk, axis=-1)
        de = down_embed[idx]
        ue = up_embed[idx]
        w = jnp.einsum('btd,bthkd->bthk', hidden_states, de)
        w = jax.nn.silu(w) * jax.nn.softmax(scores, axis=-1)
        experts_states = jnp.einsum('bthk,bthkd->btd', w, ue)
        mlp = jax.nn.silu(hidden_states @ Wg + bg) * (hidden_states @ Wu + bu) @ Wd + bd
        return mlp + experts_states
    x = L0_attn_x
    x = _layernorm(x + _L0_attn_ref(x, L0_attn_Wq, L0_attn_bq, L0_attn_Wk, L0_attn_bk, L0_attn_Wv, L0_attn_bv, L0_attn_Wo, L0_attn_bo, L0_attn_rw), axis=-1)
    x = _layernorm(x + _L0_ffn_ref(x, L0_ffn_Wg, L0_ffn_bg, L0_ffn_Wu, L0_ffn_bu, L0_ffn_Wd, L0_ffn_bd, L0_ffn_Wq, L0_ffn_keys, L0_ffn_down_embed, L0_ffn_up_embed), axis=-1)
    return x

_drawn_inputs = setup_inputs


def setup_inputs(seed=0):
    import zlib

    import numpy as np

    out = dict(_drawn_inputs(seed))
    spreads = {'L0_attn_bq': (0.0, 2.0),
     'L0_attn_bk': (0.0, 2.0),
     'L0_attn_bv': (0.0, 0.1),
     'L0_attn_bo': (0.0, 0.1),
     'L0_ffn_bg': (0.0, 0.705),
     'L0_ffn_bu': (0.0, 0.697),
     'L0_ffn_bd': (0.0, 0.1)}
    factors = {'L0_attn_rw': 71.257,
     'L0_ffn_Wq': 8.0,
     'L0_ffn_keys': 8.0,
     'L0_ffn_down_embed': 5.53,
     'L0_ffn_up_embed': 5.696,
     'L0_attn_Wq': 12.447,
     'L0_attn_Wk': 3.242}
    for name, (base, spread) in spreads.items():
        noise = np.random.default_rng([zlib.crc32(name.encode()), seed]).standard_normal(out[name].shape)
        drawn = base * np.exp(spread * noise) if base else spread * noise
        out[name] = jnp.asarray(drawn.astype(out[name].dtype))
    for name, factor in factors.items():
        out[name] = (out[name] * factor).astype(out[name].dtype)
    return out
```

```python
from contextlib import ExitStack

import concourse.bass as bass
from concourse import mybir

F32 = mybir.dt.float32
ALU = mybir.AluOpType
ACT = mybir.ActivationFunctionType
AX = mybir.AxisListType

P = 128


def block_kernel(nc, x, Wq, bq, Wk, bk, Wv, bv, Wo, bo, rw, Wg, bg, Wu, bu, Wd, bd,
                 Wrq, keys, down, up, out):
    B, S, D = x.shape
    H, DK, F = rw.shape
    KD = D // P
    HF = H * F
    FC = HF // P
    VW = 2 * DK + 1
    DFF = Wg.shape[1]
    NEXP = down.shape[0]
    C = DFF // P
    RH, NK, _, RN = keys.shape
    TOP = 8
    NX = NEXP // NK
    T = 4
    G = T * P
    NG = B * S // G
    BG = S // G
    ATTN_EPS, LN_EPS = 1e-6, 1e-5
    assert KD == 2 and FC == 8 and C == 8 and NEXP == DFF and BG == 4 and NG % 2 == 0

    ATTN_LAG, ROUTE_LAG, FFN_LAG = BG, BG + 1, BG + 2

    KV_USES = 15
    XA, KA, VA, KP, KVS = 0, 2, 4, 6, 14
    AT_USES = 22
    XQ, QQ, QP, QKV, OT, WO, XN = 0, 2, 4, 12, 16, 18, 20

    x_groups = x.rearrange("b s d -> (b s) d").rearrange("(g p t) d -> g p t d", p=P, t=T)
    out_groups = out.rearrange("b s d -> (b s) d").rearrange("(g p t) d -> g p t d", p=P, t=T)

    with ExitStack() as ctx:
        def sb(name, *shape):
            return ctx.enter_context(nc.sbuf_tensor(name, list(shape), F32))

        def ps(name):
            return ctx.enter_context(nc.psum_tensor(name, [P, G], F32))

        def sem(name):
            return ctx.enter_context(nc.semaphore(name))

        ident = sb("ident", P, P)
        wq_sb, wk_sb, wv_sb, wo_sb = (sb(n, P, KD, D) for n in ("wq_sb", "wk_sb", "wv_sb", "wo_sb"))
        rw_sb = sb("rw_sb", P, KD, G)
        wg_sb, wu_sb = sb("wg_sb", P, KD, DFF), sb("wu_sb", P, KD, DFF)
        wd_sb, up_sb = sb("wd_sb", P, C, D), sb("up_sb", P, C, D)
        downT = sb("downT", P, KD, NEXP)
        route_w = sb("route_w", P, KD, G)
        bq_sb, bk_sb = sb("bq_sb", P, KD), sb("bk_sb", P, KD)
        bg_sb, bu_sb = sb("bg_sb", P, C), sb("bu_sb", P, C)
        bv_sb, bo_sb, bd_sb = (sb(n, P, D) for n in ("bv_sb", "bo_sb", "bd_sb"))
        neg_half = sb("neg_half", P, T)
        xa = sb("xa", P, T, D)
        xaT = sb("xaT", P, KD, G)
        kT = sb("kT", P, KD, G)
        kp = sb("kp", P, T, HF)
        v_sb = sb("v_sb", P, T, FC, VW)
        kv_sum = sb("kv_sum", P, FC, VW)
        kv_blocks = sb("kv_blocks", P, FC, 2, DK + 1)
        xb = sb("xb", P, T, D)
        xbT = sb("xbT", P, KD, G)
        qT = sb("qT", P, KD, G)
        qp = sb("qp", P, FC, G)
        den = sb("den", P, T, H)
        attnT = sb("attnT", P, KD, G)
        x1 = sb("x1", P, T, D)
        stats1, mv1, rstd1 = sb("stats1", P, T, 6), sb("mv1", P, T, 2), sb("rstd1", P, T)
        x1T = sb("x1T", P, 2, KD, G)
        x1b = sb("x1b", P, 2, T, D)
        top = sb("top", P, 2 * RH, TOP)
        ex = sb("ex", P, 2 * RH, NK + TOP)
        cand = sb("cand", P, RH, TOP, TOP)
        best = sb("best", P, RH, TOP)
        zsum, rz = sb("zsum", P, RH), sb("rz", P, RH)
        grid = sb("grid", P, 3, NX, NK)
        prob = sb("prob", P, 2, T, NEXP)
        mass = sb("mass", P, 2)
        gate = sb("gate", P, 2, G)
        wexp = sb("wexp", P, 2, G)
        y_sb = sb("y_sb", P, T, D)
        stats2, mv2, rstd2 = sb("stats2", P, T, 6), sb("mv2", P, T, 2), sb("rstd2", P, T)

        kv_bank, at_bank, rt_bank = ps("kv_bank"), ps("at_bank"), ps("rt_bank")
        pt_bank = ps("pt_bank")
        ring = [ps("ring0"), ps("ring1")]
        y_bank = [ps("y_bank0"), ps("y_bank1")]

        w_loaded, rw_zero, rw_loaded = sem("w_loaded"), sem("rw_zero"), sem("rw_loaded")
        pool_prep, prep_full, prep_read = sem("pool_prep"), sem("prep_full"), sem("prep_read")
        xa_loaded = sem("xa_loaded")
        kv_full, kv_read = sem("kv_full"), sem("kv_read")
        kp_eps = sem("kp_eps")
        blocks_ready, sum_cleared = sem("blocks_ready"), sem("sum_cleared")
        xb_loaded, xb_bias = sem("xb_loaded"), sem("xb_bias")
        at_full, at_read = sem("at_full"), sem("at_read")
        qp_eps = sem("qp_eps")
        at_dve, rstd1_ready, x1_ready = sem("at_dve"), sem("rstd1_ready"), sem("x1_ready")
        ln1_pool = sem("ln1_pool")
        x1b_ready = sem("x1b_ready")
        rt_full, rt_read, rt_exp, rt_dve = sem("rt_full"), sem("rt_read"), sem("rt_exp"), sem("rt_dve")
        prob_ready = sem("prob_ready")
        ring_full, ring_act = sem("ring_full"), sem("ring_act")
        pt_full, h_ready, wexp_ready = sem("pt_full"), sem("h_ready"), sem("wexp_ready")
        y_full, y_read, y_dve = sem("y_full"), sem("y_read"), sem("y_dve")
        ln2_pool, rstd2_ready, y_ready, y_stored = (sem("ln2_pool"), sem("rstd2_ready"),
                                                    sem("y_ready"), sem("y_stored"))

        down_rows = kp[:, 0:2, :].rearrange("p a (c d) -> p (a c) d", d=D)
        wrq_rows = kp[:, 2, :].rearrange("p (k n) -> p k n", k=KD)
        keys_rows = kp[0:NK, 3, 0:2 * RH * RN].rearrange("k (a h n) -> k a h n", h=RH, a=2)
        wrqT = qp[:, 0:2, :].rearrange("p a (b d) -> p (a b) d", d=D)
        keysT = qp[:, 2, 0:4 * NK].rearrange("p (b k) -> p b k", k=NK)

        AT_STEPS = 2 * T + 2 * T
        RT_STEPS = (6 + 3 * RH + 1) * T
        Y_STEPS = 2 * T

        AT_EARLY = [[XQ], [QQ + 1], [QP + 2], [QP + 5], [QKV], [QKV + 3], [WO], []]
        AT_MID = [[XQ + 1], [QP], [QP + 3], [QP + 6], [QKV + 1], [OT], [WO + 1], []]
        AT_LATE = [[QQ], [QP + 1], [QP + 4], [QP + 7], [QKV + 2], [OT + 1], [], [XN, XN + 1]]
        KV_EARLY = [[XA], [KA], [VA], [KP], [KP + 2], [KP + 4], [KP + 6], []]
        KV_LATE = [[XA + 1], [KA + 1], [VA + 1], [KP + 1], [KP + 3], [KP + 5], [KP + 7], [KVS]]

        block = ctx.enter_context(nc.Block())

        def wait(eng, s, value):
            if not (isinstance(value, int) and value <= 0):
                eng.wait_ge(s, value)

        def wait_apart(eng, s, value):
            value = value if isinstance(value, int) else eng.to_reg(value)
            eng.wait_ge(pool_prep, 5)
            wait(eng, s, value)

        class Chain:

            def __init__(self, eng, s, group, steps):
                self.eng, self.s, self.base, self.steps, self.k = eng, s, group * steps, steps, 0

            def mark(self, ins):
                self.k += 1
                assert self.k <= self.steps
                ins.then_inc(self.s, 1)

                return self.k

            def wait(self, k=None):
                wait(self.eng, self.s, self.base + (k or self.k))

            def wait_apart(self):
                wait_apart(self.eng, self.s, self.base + self.k)

        def bcast(ap, shape):
            return ap.broadcast_to(shape)

        def schedule(eng, body, batch_end):
            def step(it, par, batch=None):
                live = lambda lag: not isinstance(it, int) or 0 <= it - lag < NG
                body(it, par, live(0), live(ATTN_LAG), live(ROUTE_LAG), live(FFN_LAG), batch)

            for it in range(2 * BG):
                step(it, it % 2, it // BG)
                if it % BG == BG - 1:
                    batch_end(it // BG)
            with eng.Fori(2, B) as b:
                with eng.Fori(0, BG // 2) as j:
                    for par in range(2):
                        step(b * BG + j * 2 + par, par, b)
                batch_end(b)
            with eng.Fori(0, BG // 2) as j:
                for par in range(2):
                    it = j * 2 + (NG + par)
                    body(it, par, False, True, True, True, B)
            for it in range(NG + BG, NG + FFN_LAG):
                step(it, it % 2, it // BG)

        W_ALL = 16 * (8 + 4 + 4 + 3)
        RW_ALL = 16 * H

        @block.sync
        def _(sp):
            def load(dst, src, by_element=False):
                sp.dma_start(dst, src, allow_slow_non_contiguous=by_element).then_inc(w_loaded, 16)

            sp.dma_start(xa[:], x_groups[0]).then_inc(xa_loaded, 16)
            for dst, src in ((wk_sb, Wk), (wv_sb, Wv), (wq_sb, Wq), (wo_sb, Wo), (wg_sb, Wg), (wu_sb, Wu),
                             (wd_sb, Wd), (up_sb, up)):
                load(dst[:], src.rearrange("(c p) n -> p c n", p=P))
            load(down_rows, down.rearrange("(c p) n -> p c n", p=P))
            load(wrq_rows, Wrq.rearrange("(c p) n -> p c n", p=P))
            for half in range(2):
                load(keys_rows[:, half], keys[:, :, half, :].rearrange("h k n -> k h n"))
            for dst, src in ((bq_sb, bq), (bk_sb, bk), (bg_sb, bg), (bu_sb, bu)):
                load(dst[:], src.rearrange("(c p) -> p c", p=P), by_element=True)
            for dst, src in ((bv_sb, bv), (bo_sb, bo), (bd_sb, bd)):
                load(dst[:], src.partition_broadcast(P))
            sp.wait_ge(rw_zero, 1)
            for h in range(H):
                half, hh = divmod(h, H // KD)
                sp.dma_start(rw_sb[DK * hh:DK * (hh + 1), half, F * hh:F * (hh + 1)],
                             rw[h]).then_inc(rw_loaded, 16)

            def body(it, par, kv, at, rt, ff, batch):
                a, m = it, it - ATTN_LAG
                if kv and not (isinstance(a, int) and a == 0):
                    wait(sp, kv_full, a * KV_USES - KV_USES + 2)
                    sp.dma_start(xa[:], x_groups[a]).then_inc(xa_loaded, 16)
                if at:
                    wait(sp, at_read, m * AT_USES - AT_USES + WO + 2)
                    sp.dma_start(xb[:], x_groups[m]).then_inc(xb_loaded, 16)

            schedule(sp, body, lambda b: None)

        @block.gpsimd
        def _(pool):
            pool.memset(rw_sb[:], 0.0).then_inc(rw_zero, 1)
            pool.memset(ident[:], 0.0).then_inc(pool_prep, 1)
            pool.memset(neg_half[:], -0.5).then_inc(pool_prep, 1)
            pool.memset(kv_blocks[:], 0.0).then_inc(pool_prep, 1)
            pool.memset(v_sb[:, :, :, 2 * DK:VW], 1.0).then_inc(pool_prep, 1)
            pool.wait_ge(pool_prep, 4)
            pool.affine_select(out=ident[:], in_=ident[:], compare_op=ALU.not_equal, fill=1.0, base=0,
                               pattern=[[-1, P]], channel_multiplier=1).then_inc(pool_prep, 1)
            pool.wait_ge(pool_prep, 5)
            pool.wait_ge(w_loaded, W_ALL)

            def norm_scale(s_dve, dve_steps, s_own, g, mv, rstd, s_out):
                wait_apart(pool, s_dve, dve_steps)
                pool.tensor_scalar(rstd[:], mv[:, :, 1], LN_EPS, None, ALU.add).then_inc(s_own, 1)
                pool.wait_ge(s_own, g + 1)
                pool.tensor_tensor(rstd[:], rstd[:], neg_half[:], ALU.pow).then_inc(s_out, 1)

            def body(it, par, kv, at, rt, ff, batch):
                a, m, s, n = it, it - ATTN_LAG, it - ROUTE_LAG, it - FFN_LAG
                if at:
                    pool.wait_ge(xb_loaded, (m + 1) * 16)
                    pool.wait_ge(at_full, m * AT_USES + XQ + 2)
                    pool.tensor_tensor(xb[:], xb[:], bcast(bo_sb[:].unsqueeze(1), [P, T, D]),
                                       ALU.add).then_inc(xb_bias, 1)
                if rt:
                    pool.wait_ge(x1_ready, (s + 1) * T)
                    wait(pool, y_read, s * 2 - 2)
                    pool.tensor_tensor(x1b[:, 1 - par], x1[:], bcast(bd_sb[:].unsqueeze(1), [P, T, D]),
                                       ALU.add).then_inc(x1b_ready, 1)
                if at:
                    for j in range(FC):
                        wait_apart(pool, at_read, m * AT_USES + QP + j + 1)
                        pool.tensor_scalar(qp[:, j], qp[:, j], ATTN_EPS, None, ALU.add).then_inc(qp_eps, 1)
                if kv:
                    for t in range(T):
                        wait_apart(pool, kv_read, a * KV_USES + KP + 2 * t + 2)
                        pool.tensor_scalar(kp[:, t], kp[:, t], ATTN_EPS, None, ALU.add).then_inc(kp_eps, 1)
                if at:
                    norm_scale(at_dve, (m + 1) * AT_STEPS, ln1_pool, m, mv1, rstd1, rstd1_ready)
                if ff:
                    norm_scale(y_dve, (n + 1) * Y_STEPS, ln2_pool, n, mv2, rstd2, rstd2_ready)
                    pool.wait_ge(y_ready, (n + 1) * T)
                    pool.dma_start(out_groups[n], y_sb[:]).then_inc(y_stored, 16)

            schedule(pool, body, lambda b: None)
            pool.wait_ge(y_stored, 16 * NG)

        @block.tensor
        def _(pe):
            pe.wait_ge(w_loaded, W_ALL)
            pe.wait_ge(rw_loaded, RW_ALL)
            pe.wait_ge(pool_prep, 5)
            banks = [kv_bank, at_bank]
            for u in range(4):
                if u >= 2:
                    pe.wait_ge(prep_read, u - 1)
                half, quad = divmod(u, 2)
                for j in range(4):
                    c = 4 * quad + j
                    mm = pe.transpose(banks[u % 2][:, j * P:(j + 1) * P],
                                      down_rows[:, c, half * P:(half + 1) * P], ident[:])
                mm.then_inc(prep_full, 1)
            for u in range(4, 6):
                pe.wait_ge(prep_read, u - 1)
                half = u - 4
                for b in range(4):
                    mm = pe.transpose(banks[u % 2][:, b * P:(b + 1) * P],
                                      wrq_rows[:, half, b * P:(b + 1) * P], ident[:])
                mm.then_inc(prep_full, 1)
            pe.wait_ge(prep_read, 5)
            for b in range(4):
                mm = pe.transpose(banks[0][:, b * NK:(b + 1) * NK],
                                  keys_rows[:, b // 2, 2 * (b % 2):2 * (b % 2) + 2, :].rearrange("k h n -> k (h n)"),
                                  ident[0:NK, 0:NK])
            mm.then_inc(prep_full, 1)
            pe.wait_ge(prep_read, 7)
            for g2 in range(2):
                r = slice(g2 * RN, (g2 + 1) * RN)
                for half in range(KD):
                    for b in range(4):
                        col = (half * 4 + b) * NK
                        mm = pe.matmul(banks[1 - g2][:, col:col + NK], wrqT[r, b, half * P:(half + 1) * P],
                                       keysT[r, b, :], start=True, stop=True)
                mm.then_inc(prep_full, 1)
            pe.wait_ge(prep_read, 9)

            def body(it, par, kv, at, rt, ff, batch):
                a, m, s, n = it, it - ATTN_LAG, it - ROUTE_LAG, it - FFN_LAG
                other = 1 - par

                def turn(bank, src, half):
                    for t in range(T):
                        mm = pe.transpose(bank[:, t * P:(t + 1) * P], src[:, t, half * P:(half + 1) * P], ident[:])
                    return mm

                def project(bank, w, srcT, e):
                    for k in range(KD):
                        mm = pe.matmul(bank[:], w[:, k, e * P:(e + 1) * P], srcT[:, k, :],
                                       start=(k == 0), stop=(k == KD - 1))
                    return mm

                def project_rows(bank, srcT, w, t0):
                    for t in (t0, t0 + 1):
                        for k in range(KD):
                            mm = pe.matmul(bank[:, (t - t0) * D:(t - t0 + 1) * D],
                                           srcT[:, k, t * P:(t + 1) * P], w[:, k, :],
                                           start=(k == 0), stop=(k == KD - 1))
                    return mm

                def kv_use(u):
                    wait(pe, kv_read, a * KV_USES + u)
                    if u < KA:
                        if u == XA:
                            pe.wait_ge(xa_loaded, (a + 1) * 16)
                        mm = turn(kv_bank, xa, u - XA)
                    elif u < VA:
                        mm = project(kv_bank, wk_sb, xaT, u - KA)
                    elif u < KP:
                        mm = project_rows(kv_bank, xaT, wv_sb, 2 * (u - VA))
                    elif u < KVS:
                        t, half = divmod(u - KP, 2)
                        mm = pe.matmul(kv_bank[:], kT[:, half, t * P:(t + 1) * P], rw_sb[:, half, :],
                                       start=True, stop=True)
                    else:
                        pe.wait_ge(kp_eps, (a + 1) * T)
                        for c in range(FC):
                            for t in range(T):
                                mm = pe.matmul(kv_bank[:, c * VW:(c + 1) * VW], kp[:, t, c * P:(c + 1) * P],
                                               v_sb[:, t, c, :], start=(t == 0), stop=(t == T - 1))
                    mm.then_inc(kv_full, 1)

                def at_use(u):
                    wait(pe, at_read, m * AT_USES + u)
                    if u < QQ:
                        if u == XQ:
                            pe.wait_ge(xb_loaded, (m + 1) * 16)
                        mm = turn(at_bank, xb, u - XQ)
                    elif u < QP:
                        mm = project(at_bank, wq_sb, xbT, u - QQ)
                    elif u < QKV:
                        half, c = divmod(u - QP, FC // 2)
                        mm = pe.matmul(at_bank[:], rw_sb[:, half, c * P:(c + 1) * P], qT[:, half, :],
                                       start=True, stop=True)
                    elif u < OT:
                        t = u - QKV
                        if t == 0:
                            pe.wait_ge(qp_eps, (m + 1) * FC)
                            pe.wait_ge(blocks_ready, batch)
                        for c in range(FC):
                            mm = pe.matmul(at_bank[:, c * 2 * (DK + 1):(c + 1) * 2 * (DK + 1)],
                                           qp[:, c, t * P:(t + 1) * P],
                                           kv_blocks[:, c].rearrange("p a b -> p (a b)"), start=True, stop=True)
                    elif u < WO:
                        mm = turn(at_bank, x1, u - OT)
                    elif u < XN:
                        mm = project_rows(at_bank, attnT, wo_sb, 2 * (u - WO))
                    else:
                        pe.wait_ge(x1_ready, (m + 1) * T)
                        mm = turn(at_bank, x1, u - XN)
                    mm.then_inc(at_full, 1)

                def rt_use(t):
                    if t == 0:
                        pe.wait_ge(at_read, (s + 1) * AT_USES)
                    wait(pe, rt_read, s * T + t)
                    for k in range(KD):
                        mm = pe.matmul(rt_bank[:], x1T[:, other, k, t * P:(t + 1) * P], route_w[:, k, :],
                                       start=(k == 0), stop=(k == KD - 1))
                    mm.then_inc(rt_full, 1)

                def ff_gate(c):
                    wait(pe, h_ready, n * C + c)
                    project(ring[c % 2], wg_sb, x1T[:, par], c).then_inc(ring_full, 1)

                def ff_up(c):
                    wait(pe, ring_act, (n * C + c) * 2)
                    project(ring[1 - c % 2], wu_sb, x1T[:, par], c).then_inc(ring_full, 1)

                def ff_dots(c):
                    pe.wait_ge(ring_act, (n * C + c) * 2 + 1)
                    project(ring[c % 2], downT, x1T[:, par], c).then_inc(ring_full, 1)

                def ff_weights(c):
                    wait(pe, wexp_ready, n * C + c)
                    if c == 0:
                        pe.wait_ge(prob_ready, (n + 1) * T)
                    for t in range(T):
                        mm = pe.transpose(pt_bank[:, t * P:(t + 1) * P], prob[:, par, t, c * P:(c + 1) * P],
                                          ident[:])
                    mm.then_inc(pt_full, 1)

                def ff_out(c, pair):
                    if pair == 0:
                        if c == 0:
                            wait(pe, y_read, n * 2)
                        pe.wait_ge(h_ready, n * C + c + 1)
                        pe.wait_ge(wexp_ready, n * C + c + 1)
                    for t in (2 * pair, 2 * pair + 1):
                        rows = y_bank[pair][:, (t % 2) * D:(t % 2 + 1) * D]
                        pe.matmul(rows, gate[:, c % 2, t * P:(t + 1) * P], wd_sb[:, c, :],
                                  start=(c == 0 and t % 2 == 0), stop=False, skip_group_check=True)
                        mm = pe.matmul(rows, wexp[:, c % 2, t * P:(t + 1) * P], up_sb[:, c, :],
                                       start=False, stop=(c == C - 1), skip_group_check=True)
                    if pair == 1:
                        mm.then_inc(y_full, 1)

                for c in range(C):
                    if ff:
                        ff_gate(c)
                    if at:
                        for u in AT_EARLY[c]:
                            at_use(u)
                    if ff:
                        ff_up(c)
                    if kv:
                        for u in KV_EARLY[c]:
                            kv_use(u)
                    if rt and c % 2 == 0:
                        rt_use(c // 2)
                    if ff:
                        ff_dots(c)
                    if at:
                        for u in AT_MID[c]:
                            at_use(u)
                    if ff:
                        ff_weights(c)
                        if c:
                            ff_out(c - 1, 0)
                    if kv:
                        for u in KV_LATE[c]:
                            kv_use(u)
                    if ff and c:
                        ff_out(c - 1, 1)
                    if at:
                        for u in AT_LATE[c]:
                            at_use(u)
                if ff:
                    ff_out(C - 1, 0)
                    ff_out(C - 1, 1)

            schedule(pe, body, lambda b: None)

        @block.scalar
        def _(act):
            banks = [kv_bank, at_bank]
            for u in range(9):
                act.wait_ge(prep_full, u + 1)
                bank = banks[u % 2]
                if u < 4:
                    half, quad = divmod(u, 2)
                    ins = act.copy(downT[:, half, quad * G:(quad + 1) * G], bank[:])
                elif u < 6:
                    ins = act.copy(wrqT[:, :, (u - 4) * P:(u - 3) * P],
                                   bank[:].rearrange("p (b d) -> p b d", b=4))
                elif u == 6:
                    ins = act.copy(keysT, bank[:, 0:4 * NK].rearrange("p (b k) -> p b k", k=NK))
                else:
                    ins = act.copy(route_w[:].rearrange("p k (b g n) -> p (k b) g n", b=4, g=2)[:, :, u - 7, :],
                                   bank[:].rearrange("p (b n) -> p b n", n=NK))
                ins.then_inc(prep_read, 1)
            act.wait_ge(w_loaded, W_ALL)

            def body(it, par, kv, at, rt, ff, batch):
                a, m, s, n = it, it - ATTN_LAG, it - ROUTE_LAG, it - FFN_LAG

                def kv_use(u):
                    if VA <= u < KP or u == KVS:
                        return
                    act.wait_ge(kv_full, a * KV_USES + u + 1)
                    if u < KA:
                        ins = act.copy(xaT[:, u - XA, :], kv_bank[:])
                    elif u < VA:
                        ins = act.activation(kT[:, u - KA, :], kv_bank[:], ACT.Identity,
                                             bias=bk_sb[:, u - KA:u - KA + 1])
                    else:
                        t, half = divmod(u - KP, 2)
                        ins = act.activation(kp[:, t, half * G:(half + 1) * G], kv_bank[:], ACT.Relu)
                    ins.then_inc(kv_read, 1)

                def at_use(u):
                    if QKV <= u < OT or WO <= u < XN:
                        return
                    act.wait_ge(at_full, m * AT_USES + u + 1)
                    if u < QQ:
                        ins = act.copy(xbT[:, u - XQ, :], at_bank[:])
                    elif u < QP:
                        ins = act.activation(qT[:, u - QQ, :], at_bank[:], ACT.Identity,
                                             bias=bq_sb[:, u - QQ:u - QQ + 1])
                    elif u < QKV:
                        ins = act.activation(qp[:, u - QP, :], at_bank[:], ACT.Relu)
                    elif u < WO:
                        ins = act.copy(attnT[:, u - OT, :], at_bank[:])
                    else:
                        ins = act.copy(x1T[:, par, u - XN, :], at_bank[:])
                    ins.then_inc(at_read, 1)

                def rt_use(t):
                    act.wait_ge(rt_read, s * T + t + 1)
                    act.wait_ge(rt_dve, s * RT_STEPS + t * (RT_STEPS // T) + 2)
                    act.activation(ex[:], ex[:], ACT.Exp).then_inc(rt_exp, 1)

                def ff_gate(c):
                    act.wait_ge(ring_full, n * (3 * C) + 3 * c + 1)
                    wait(act, y_full, n * C + c - 1)
                    act.activation(gate[:, c % 2], ring[c % 2][:], ACT.Silu,
                                   bias=bg_sb[:, c:c + 1]).then_inc(ring_act, 1)

                def ff_dots(c):
                    act.wait_ge(ring_full, n * (3 * C) + 3 * c + 3)
                    act.activation(wexp[:, c % 2], ring[c % 2][:], ACT.Silu).then_inc(ring_act, 1)

                for c in range(C):
                    if ff:
                        ff_gate(c)
                    if at:
                        for u in AT_EARLY[c]:
                            at_use(u)
                    if kv:
                        for u in KV_EARLY[c]:
                            kv_use(u)
                    if ff:
                        ff_dots(c)
                    if rt and c % 2 == 0:
                        rt_use(c // 2)
                    if at:
                        for u in AT_MID[c]:
                            at_use(u)
                    if kv:
                        for u in KV_LATE[c]:
                            kv_use(u)
                    if at:
                        for u in AT_LATE[c]:
                            at_use(u)

            schedule(act, body, lambda b: None)

        @block.vector
        def _(dve):
            dve.memset(kv_sum[:], 0.0).then_inc(sum_cleared, 1)
            dve.wait_ge(pool_prep, 5)
            dve.wait_ge(w_loaded, W_ALL)

            def pair(bank):
                return bank[:].rearrange("p (t d) -> p t d", t=2)

            def body(it, par, kv, at, rt, ff, batch):
                a, m, s, n = it, it - ATTN_LAG, it - ROUTE_LAG, it - FFN_LAG
                other = 1 - par
                at_steps = Chain(dve, at_dve, m, AT_STEPS)
                rt_steps = Chain(dve, rt_dve, s, RT_STEPS)
                y_steps = Chain(dve, y_dve, n, Y_STEPS)
                marks = {}

                def statistics(rows, stats, mv, steps):
                    for t in range(T):
                        steps.mark(dve.bn_stats(stats[:, t, :], rows[:, t, :]))
                    steps.wait_apart()
                    for t in range(T):
                        steps.mark(dve.bn_aggr(mv[:, t, :], stats[:, t, :]))

                def kv_use(u):
                    if VA <= u < KP:
                        i = u - VA
                        dve.wait_ge(kv_full, a * KV_USES + u + 1)
                        dve.tensor_tensor(v_sb[:, 2 * i:2 * i + 2, :, 0:2 * DK],
                                          kv_bank[:].rearrange("p (t c w) -> p t c w", t=2, c=FC),
                                          bcast(bv_sb[:].rearrange("p (c w) -> p c w", c=FC).unsqueeze(1),
                                                [P, 2, FC, 2 * DK]), ALU.add).then_inc(kv_read, 1)
                    elif u == KVS:
                        dve.wait_ge(kv_full, a * KV_USES + u + 1)
                        dve.wait_ge(sum_cleared, batch + 1)
                        dve.tensor_tensor(kv_sum[:], kv_bank[:, 0:FC * VW].rearrange("p (c w) -> p c w", c=FC),
                                          kv_sum[:], ALU.add).then_inc(kv_read, 1)

                def at_use(u):
                    if QKV <= u < OT:
                        t = u - QKV
                        if t == 0:
                            wait(dve, x1b_ready, m)
                        heads = at_bank[:, 0:H * (DK + 1)].rearrange("p (h w) -> p h w", h=H)
                        dve.wait_ge(at_full, m * AT_USES + u + 1)
                        at_steps.mark(dve.tensor_scalar(den[:, t, :], heads[:, :, DK], ATTN_EPS, None, ALU.add))
                        at_steps.wait()
                        at_steps.mark(dve.reciprocal(den[:, t, :], den[:, t, :]))
                        at_steps.wait()
                        dve.tensor_tensor(x1[:, t, :].rearrange("p (h w) -> p h w", h=H), heads[:, :, 0:DK],
                                          bcast(den[:, t, :].unsqueeze(2), [P, H, DK]),
                                          ALU.mult).then_inc(at_read, 1)
                    elif WO <= u < XN:
                        i = u - WO
                        if i == 0:
                            dve.wait_ge(xb_bias, m + 1)
                        dve.wait_ge(at_full, m * AT_USES + u + 1)
                        dve.tensor_tensor(x1[:, 2 * i:2 * i + 2, :], pair(at_bank), xb[:, 2 * i:2 * i + 2, :],
                                          ALU.add).then_inc(at_read, 1)

                def norm1_stats():
                    dve.wait_ge(at_read, m * AT_USES + WO + 2)
                    statistics(x1, stats1, mv1, at_steps)

                def norm1():
                    dve.wait_ge(rstd1_ready, m + 1)
                    for t in range(T):
                        dve.tensor_scalar(x1[:, t, :], x1[:, t, :], mv1[:, t, 0:1], rstd1[:, t:t + 1],
                                          ALU.subtract, ALU.mult).then_inc(x1_ready, 1)

                def scores(t):
                    rt_steps.wait()
                    wait_apart(dve, rt_full, s * T + t + 1)
                    for g in range(2 * RH):
                        ins = dve.max(top[:, g, :], rt_bank[:, g * NK:(g + 1) * NK])
                    rt_steps.mark(ins)
                    rt_steps.wait()
                    dve.tensor_tensor(ex[:, :, 0:NK], rt_bank[:].rearrange("p (g k) -> p g k", k=NK),
                                      bcast(top[:, :, 0:1], [P, 2 * RH, NK]), ALU.subtract).then_inc(rt_read, 1)
                    rt_steps.mark(dve.tensor_tensor(ex[:, :, NK:], top[:], bcast(top[:, :, 0:1], [P, 2 * RH, TOP]),
                                                    ALU.subtract))

                def choose(t):
                    dve.wait_ge(rt_exp, s * T + t + 1)
                    rt_steps.mark(dve.tensor_tensor(
                        cand[:], bcast(ex[:, 0:RH, NK:].unsqueeze(3), [P, RH, TOP, TOP]),
                        bcast(ex[:, RH:, NK:].unsqueeze(2), [P, RH, TOP, TOP]), ALU.mult))
                    rt_steps.wait_apart()
                    for h in range(RH):
                        ins = dve.max(best[:, h, :], cand[:, h].rearrange("p a b -> p (a b)"))
                    rt_steps.mark(ins)
                    rt_steps.wait()
                    rt_steps.mark(dve.reduce_sum(zsum[:], best[:], AX.X))
                    rt_steps.wait()
                    marks["rz"] = rt_steps.mark(dve.reciprocal(rz[:], zsum[:]))

                def spread(t, h):
                    if h == 3:
                        rt_steps.wait(marks["add", 0])
                    marks["spread", h] = rt_steps.mark(dve.tensor_tensor(
                        grid[:, h % 3], bcast(ex[:, h, 0:NX].unsqueeze(2), [P, NX, NK]),
                        bcast(ex[:, RH + h, 0:NK].unsqueeze(1), [P, NX, NK]), ALU.mult))

                def keep(t, h):
                    rt_steps.wait(marks["spread", h])
                    g = grid[:, h % 3].rearrange("p a b -> p (a b)")
                    marks["keep", h] = rt_steps.mark(dve.scalar_tensor_tensor(
                        out=g, in0=g, scalar=best[:, h, TOP - 1:TOP], in1=g, op0=ALU.is_ge, op1=ALU.mult))

                def add_head(t, h):
                    g = grid[:, h % 3].rearrange("p a b -> p (a b)")
                    row = prob[:, other, t, :]
                    rt_steps.wait(marks["keep", h])
                    if h == 0:
                        rt_steps.wait(max(marks["rz"], marks["keep", h]))
                        if t == 0:
                            wait(dve, pt_full, (s - 1) * C)
                        ins = dve.tensor_scalar(row, g, rz[:, 0:1], None, ALU.mult)
                    else:
                        rt_steps.wait(marks["add", h - 1])
                        ins = dve.scalar_tensor_tensor(out=row, in0=g, scalar=rz[:, h:h + 1], in1=row,
                                                       op0=ALU.mult, op1=ALU.add,
                                                       accum_out=mass[:, 0:1] if h == RH - 1 else None)
                    marks["add", h] = rt_steps.mark(ins)

                def clamp(t):
                    rt_steps.wait()
                    rt_steps.mark(dve.tensor_scalar(mass[:, 1:2], mass[:, 0:1], -1.0, float(RH), ALU.mult, ALU.add))
                    rt_steps.wait()
                    last = prob[:, other, t, NEXP - 1:NEXP]
                    dve.tensor_tensor(last, last, mass[:, 1:2], ALU.add).then_inc(prob_ready, 1)

                def ff_h(c):
                    dve.wait_ge(ring_full, n * (3 * C) + 3 * c + 2)
                    dve.wait_ge(ring_act, n * (2 * C) + 2 * c + 1)
                    dve.scalar_tensor_tensor(out=gate[:, c % 2], in0=ring[1 - c % 2][:], scalar=bu_sb[:, c:c + 1],
                                             in1=gate[:, c % 2], op0=ALU.add, op1=ALU.mult).then_inc(h_ready, 1)

                def ff_wexp(c):
                    dve.wait_ge(pt_full, n * C + c + 1)
                    dve.wait_ge(ring_act, n * (2 * C) + 2 * c + 2)
                    dve.tensor_tensor(wexp[:, c % 2], pt_bank[:], wexp[:, c % 2], ALU.mult).then_inc(wexp_ready, 1)

                def finish():
                    dve.wait_ge(y_full, (n + 1) * C)
                    dve.wait_ge(x1b_ready, n + 1)
                    wait(dve, y_stored, n * 16)
                    for i in range(2):
                        dve.tensor_tensor(y_sb[:, 2 * i:2 * i + 2, :], pair(y_bank[i]),
                                          x1b[:, par, 2 * i:2 * i + 2, :], ALU.add).then_inc(y_read, 1)
                    dve.wait_ge(y_read, (n + 1) * 2)
                    statistics(y_sb, stats2, mv2, y_steps)
                    dve.wait_ge(rstd2_ready, n + 1)
                    for t in range(T):
                        dve.tensor_scalar(y_sb[:, t, :], y_sb[:, t, :], mv2[:, t, 0:1], rstd2[:, t:t + 1],
                                          ALU.subtract, ALU.mult).then_inc(y_ready, 1)

                for c in range(C):
                    t = c // 2
                    if at:
                        for u in AT_EARLY[c]:
                            at_use(u)
                    if rt and c % 2 == 1:
                        spread(t, 2), keep(t, 1), add_head(t, 0)
                    if ff:
                        ff_h(c)
                    if kv:
                        for u in KV_EARLY[c]:
                            kv_use(u)
                    if rt and c % 2 == 0:
                        scores(t)
                    if rt and c % 2 == 1:
                        spread(t, 3), keep(t, 2), add_head(t, 1)
                    if at:
                        for u in AT_MID[c]:
                            at_use(u)
                        if c == 6:
                            norm1_stats()
                    if ff:
                        ff_wexp(c)
                    if rt and c % 2 == 1:
                        keep(t, 3), add_head(t, 2)
                    if kv:
                        for u in KV_LATE[c]:
                            kv_use(u)
                    if at and c == 7:
                        norm1()
                    if rt and c % 2 == 1:
                        add_head(t, 3), clamp(t)
                    if rt and c % 2 == 0:
                        choose(t), spread(t, 0), spread(t, 1), keep(t, 0)
                    if at:
                        for u in AT_LATE[c]:
                            at_use(u)
                if ff:
                    finish()
                assert not rt or rt_steps.k == RT_STEPS

            def batch_end(b):
                dve.wait_ge(kv_read, (b + 1) * (BG * KV_USES))
                for g2 in range(2):
                    rows = slice(g2 * F, (g2 + 1) * F)
                    dve.tensor_copy(kv_blocks[rows, :, g2, 0:DK], kv_sum[rows, :, g2 * DK:(g2 + 1) * DK])
                    ins = dve.tensor_copy(kv_blocks[rows, :, g2, DK:DK + 1], kv_sum[rows, :, 2 * DK:VW])
                ins.then_inc(blocks_ready, 1)
                dve.wait_ge(blocks_ready, b + 1)
                dve.memset(kv_sum[:], 0.0).then_inc(sum_cleared, 1)

            schedule(dve, body, batch_end)


_INS = ["x", "Wq", "bq", "Wk", "bk", "Wv", "bv", "Wo", "bo", "rw"]
_FFN = ["Wg", "bg", "Wu", "bu", "Wd", "bd", "Wq", "keys", "down_embed", "up_embed"]


def kernel(**inputs):
    import numpy as _np
    import concourse.bacc as _bacc
    from concourse import mybir as _mybir
    from concourse.bass_utils import run_bass_kernel_spmd as _run

    nc = _bacc.Bacc("TRN2", target_bir_lowering=False, num_devices=1)
    arrays, args = {}, []
    for name in [f"L0_attn_{n}" for n in _INS] + [f"L0_ffn_{n}" for n in _FFN]:
        a = _np.ascontiguousarray(inputs[name])
        arrays[f"in_{name}"] = a
        args.append(nc.dram_tensor(f"in_{name}", a.shape, _mybir.dt.from_np(a.dtype), kind="ExternalInput").ap())
    shape = inputs["L0_attn_x"].shape
    args.append(nc.dram_tensor("out_y", shape, _mybir.dt.float32, kind="ExternalOutput").ap())
    block_kernel(nc, *args)
    r = _run(nc, [arrays], core_ids=[0])
    return r.results[0]["out_y"]
```

```python
from contextlib import ExitStack

import concourse.bass as bass
from concourse import mybir

F32 = mybir.dt.float32
F32R = mybir.dt.float32r
ALU = mybir.AluOpType
ACT = mybir.ActivationFunctionType
AX = mybir.AxisListType

P = 128


def block_kernel(nc, x, Wq, bq, Wk, bk, Wv, bv, Wo, bo, rw, Wg, bg, Wu, bu, Wd, bd,
                 Wrq, keys, down, up, out):
    B, S, D = x.shape
    H, DK, F = rw.shape
    KD = D // P
    HF = H * F
    FC = HF // P
    VW = 2 * DK + 1
    DFF = Wg.shape[1]
    NEXP = down.shape[0]
    C = DFF // P
    RH, NK, _, RN = keys.shape
    TOP = 8
    NX = NEXP // NK
    T = 4
    G = T * P
    NG = B * S // G
    BG = S // G
    ATTN_EPS, LN_EPS = 1e-6, 1e-5
    assert KD == 2 and FC == 8 and C == 8 and NEXP == DFF and BG == 4 and NG % 2 == 0

    ATTN_LAG, ROUTE_LAG, FFN_LAG, LAST_LAG = BG, BG + 1, BG + 2, BG + 3

    KV_TILE = [[("kp", 2 * t), ("kp", 2 * t + 1), ("sum", t)] for t in range(T)]
    KV_SEQ = ([("turn", 0), ("turn", 1), ("k", 0), ("k", 1), ("v", 0)] + KV_TILE[0] + KV_TILE[1]
              + [("v", 1)] + KV_TILE[2] + KV_TILE[3])
    AT_SEQ = ([("turn", 0), ("turn", 1), ("q", 0), ("q", 1)] + [("qp", j) for j in range(4)] + [("qkv", 0)]
              + [("qp", 4), ("qp", 5), ("qkv", 1), ("qp", 6), ("qp", 7), ("qkv", 2), ("qkv", 3)]
              + [("back", 0), ("back", 1), ("wo", 0), ("wo", 1), ("next", 0), ("next", 1)])
    KV_USES, AT_USES = len(KV_SEQ), len(AT_SEQ)
    KV_U = {use: u for u, use in enumerate(KV_SEQ)}
    AT_U = {use: u for u, use in enumerate(AT_SEQ)}

    x_groups = x.rearrange("b s d -> (b s) d").rearrange("(g p t) d -> g p t d", p=P, t=T)
    out_groups = out.rearrange("b s d -> (b s) d").rearrange("(g p t) d -> g p t d", p=P, t=T)

    with ExitStack() as ctx:
        def sb(name, *shape, dt=F32):
            return ctx.enter_context(nc.sbuf_tensor(name, list(shape), dt))

        def ps(name):
            return ctx.enter_context(nc.psum_tensor(name, [P, G], F32))

        def sem(name):
            return ctx.enter_context(nc.semaphore(name))

        wq_sb, wk_sb, wv_sb, wo_sb = (sb(n, P, KD, D) for n in ("wq_sb", "wk_sb", "wv_sb", "wo_sb"))
        rw_hl = sb("rw_hl", P, 2, 2 * KD, G // 2, dt=F32R)
        wg_hl, wu_hl, downT_hl = (sb(n, P, 2, KD, DFF, dt=F32R) for n in ("wg_hl", "wu_hl", "downT_hl"))
        route_hl = sb("route_hl", P, 2, KD, G, dt=F32R)
        ident_r = sb("ident_r", P, P, dt=F32R)
        ident = ident_r[:].bitcast(F32)
        wd_sb, up_sb = sb("wd_sb", P, C, D), sb("up_sb", P, C, D)
        bq_sb, bk_sb = sb("bq_sb", P, KD), sb("bk_sb", P, KD)
        bg_sb, bu_sb = sb("bg_sb", P, C), sb("bu_sb", P, C)
        bv_sb, bo_sb, bd_sb = (sb(n, P, D) for n in ("bv_sb", "bo_sb", "bd_sb"))
        neg_half = sb("neg_half", P, T)
        xa = sb("xa", P, T, D)
        xaT = sb("xaT", P, KD, G)
        kT_hl = sb("kT_hl", P, 2 * KD, G, dt=F32R)
        kp = sb("kp", P, HF)
        v_sb = sb("v_sb", P, 2, FC, VW)
        kv_sum = sb("kv_sum", P, FC, VW)
        kv_blocks = sb("kv_blocks", P, FC, 2, DK + 1)
        xb = sb("xb", P, T, D)
        qT_hl = sb("qT_hl", P, 2 * KD, G, dt=F32R)
        qp = sb("qp", P, 4, G)
        xbT = qp[:, 2:4]
        den = sb("den", P, T, 4)
        attnT = xbT
        x1 = sb("x1", P, T, D)
        stats, mv1, rstd1 = sb("stats", P, T, 6), sb("mv1", P, T, 2), sb("rstd1", P, T)
        x1T_hl = sb("x1T_hl", P, 2, 2, KD, G, dt=F32R)
        top = sb("top", P, 2 * RH, TOP)
        ex = sb("ex", P, 2 * RH, NK + TOP)
        cand = sb("cand", P, RH, TOP, TOP)
        best = sb("best", P, RH, TOP)
        zsum, rz = sb("zsum", P, RH), sb("rz", P, RH)
        grid = sb("grid", P, 2, NX, NK)
        prob = sb("prob", P, 2, T, NEXP)
        mass = sb("mass", P, 2)
        gate = sb("gate", P, 2, G)
        wexp = sb("wexp", P, 2, G)
        y_sb = x1
        mv2, rstd2 = sb("mv2", P, T, 2), sb("rstd2", P, T)

        kv_bank, at_bank, rt_bank = ps("kv_bank"), ps("at_bank"), ps("rt_bank")
        pt_bank = ps("pt_bank")
        ring = [ps("ring0"), ps("ring1")]
        y_bank = [ps("y_bank0"), ps("y_bank1")]

        w_loaded, rw_zero, rw_loaded = sem("w_loaded"), sem("rw_zero"), sem("rw_loaded")
        pool_prep, prep_full, prep_read = sem("pool_prep"), sem("prep_full"), sem("prep_read")
        high_ready, low_ready, prep_low = sem("high_ready"), sem("low_ready"), sem("prep_low")
        rw_high = sem("rw_high")
        xa_loaded = sem("xa_loaded")
        kv_full, kv_read = sem("kv_full"), sem("kv_read")
        k_high, kp_eps = sem("k_high"), sem("kp_eps")
        blocks_ready, sum_cleared = sem("blocks_ready"), sem("sum_cleared")
        xb_loaded, xb_bias, x1_high = sem("xb_loaded"), sem("xb_bias"), sem("x1_high")
        at_full, at_read = sem("at_full"), sem("at_read")
        q_high, qp_eps = sem("q_high"), sem("qp_eps")
        at_dve, rstd1_ready, x1_ready = sem("at_dve"), sem("rstd1_ready"), sem("x1_ready")
        ln1_pool = sem("ln1_pool")
        rt_full, rt_read, rt_exp, rt_dve = sem("rt_full"), sem("rt_read"), sem("rt_exp"), sem("rt_dve")
        spread_ready, prob_ready = sem("spread_ready"), sem("prob_ready")
        ring_full, ring_act = sem("ring_full"), sem("ring_act")
        pt_full, h_ready, wexp_ready = sem("pt_full"), sem("h_ready"), sem("wexp_ready")
        y_full, y_read, y_dve = sem("y_full"), sem("y_read"), sem("y_dve")
        ln2_pool, rstd2_ready, y_ready, y_stored = (sem("ln2_pool"), sem("rstd2_ready"),
                                                    sem("y_ready"), sem("y_stored"))

        AT_STEPS = 2 * T + 2 * T
        RT_TILE = ["top", "less", "cand", "best", "sum", "rz", ("keep", 0), ("keep", 1), ("add", 0), ("keep", 2),
                   ("add", 1), ("keep", 3), ("add", 2), ("add", 3), "mass"]
        RT_AT = {name: k + 1 for k, name in enumerate(RT_TILE)}
        RT_STEPS = len(RT_TILE) * T
        Y_STEPS = 2 * T

        AT_EARLY = [AT_SEQ[3 * c:3 * c + 1] for c in range(7)] + [[]]
        AT_MID = [AT_SEQ[3 * c + 1:3 * c + 2] if c < 6 else [] for c in range(7)] + [[]]
        AT_LATE = [AT_SEQ[3 * c + 2:3 * c + 3] for c in range(6)] + [[], AT_SEQ[-2:]]
        AT_MID[6] = [("wo", 1)]
        kv_places, left = [(c, place) for c in range(C) for place in range(3) if place or c in (3, 6)], iter(KV_SEQ)
        kv_place = {at: [next(left)] for at in kv_places}
        KV_FIRST, KV_EARLY, KV_LATE = ([kv_place.get((c, place), []) for c in range(C)] for place in range(3))

        stage = prob[:].rearrange("p a t e -> p (a t e)")
        cut = lambda at, n: stage[:, at:at + n]
        down_rows = cut(0, C * D).rearrange("p (c d) -> p c d", d=D)
        wg_rows = cut(C * D, KD * DFF).rearrange("p (k n) -> p k n", k=KD)
        wu_rows = cut(C * D + KD * DFF, KD * DFF).rearrange("p (k n) -> p k n", k=KD)
        wrq_rows = cut(C * D + 2 * KD * DFF, KD * G).rearrange("p (k n) -> p k n", k=KD)
        keys_rows = cut(C * D + 2 * KD * DFF + KD * G, 2 * RH * RN)[0:NK].rearrange("k (a h n) -> k a h n", h=RH, a=2)
        wrqT = x1[:]
        stage2 = grid[:].rearrange("p g a b -> p (g a b)")
        rw_rows = stage2[:, 0:KD * G].rearrange("p (b n) -> p b n", b=2 * KD)
        ident_rows = stage2[:, KD * G:KD * G + P]
        keysT = stage2[:, KD * G + P:KD * G + P + 4 * NK].rearrange("p (b k) -> p b k", k=NK)

        def route_half(part, g2):
            return route_hl[:, part].rearrange("p k (b g n) -> p (k b) g n", b=4, g=2)[:, :, g2, :]

        block = ctx.enter_context(nc.Block())

        def wait(eng, s, value):
            if not (isinstance(value, int) and value <= 0):
                eng.wait_ge(s, value)

        def wait_apart(eng, s, value):
            value = value if isinstance(value, int) else eng.to_reg(value)
            eng.wait_ge(pool_prep, 5)
            wait(eng, s, value)

        class Chain:

            def __init__(self, eng, s, group, steps):
                self.eng, self.s, self.base, self.steps, self.k = eng, s, group * steps, steps, 0

            def mark(self, ins):
                self.k += 1
                assert self.k <= self.steps
                ins.then_inc(self.s, 1)

                return self.k

            def wait(self, k=None):
                wait(self.eng, self.s, self.base + (k or self.k))

            def wait_apart(self):
                wait_apart(self.eng, self.s, self.base + self.k)

        def bcast(ap, shape):
            return ap.broadcast_to(shape)

        def schedule(eng, body, batch_end):
            def step(it, par, batch=None):
                live = lambda lag: not isinstance(it, int) or 0 <= it - lag < NG
                body(it, par, live(0), live(ATTN_LAG), live(ROUTE_LAG), live(FFN_LAG), live(LAST_LAG), batch)

            for it in range(2 * BG):
                step(it, it % 2, it // BG)
                if it % BG == BG - 1:
                    batch_end(it // BG)
            with eng.Fori(2, B) as b:
                with eng.Fori(0, BG // 2) as j:
                    for par in range(2):
                        step(b * BG + j * 2 + par, par, b)
                batch_end(b)
            with eng.Fori(0, BG // 2) as j:
                for par in range(2):
                    it = j * 2 + (NG + par)
                    body(it, par, False, True, True, True, True, B)
            for it in range(NG + BG, NG + LAST_LAG):
                step(it, it % 2, it // BG)

        W_ALL = 16 * (8 + 4 + 4 + 3)
        RW_ALL = 16 * 8

        @block.sync
        def _(sp):
            def load(dst, src, by_element=False):
                sp.dma_start(dst, src, allow_slow_non_contiguous=by_element).then_inc(w_loaded, 16)

            sp.dma_start(xa[:], x_groups[0]).then_inc(xa_loaded, 16)
            for dst, src in ((wk_sb, Wk), (wv_sb, Wv), (wq_sb, Wq), (wo_sb, Wo), (wd_sb, Wd), (up_sb, up)):
                load(dst[:], src.rearrange("(c p) n -> p c n", p=P))
            load(wg_rows, Wg.rearrange("(c p) n -> p c n", p=P))
            load(wu_rows, Wu.rearrange("(c p) n -> p c n", p=P))
            load(down_rows, down.rearrange("(c p) n -> p c n", p=P))
            load(wrq_rows, Wrq.rearrange("(c p) n -> p c n", p=P))
            for half in range(2):
                load(keys_rows[:, half], keys[:, :, half, :].rearrange("h k n -> k h n"))
            for dst, src in ((bq_sb, bq), (bk_sb, bk), (bg_sb, bg), (bu_sb, bu)):
                load(dst[:], src.rearrange("(c p) -> p c", p=P), by_element=True)
            for dst, src in ((bv_sb, bv), (bo_sb, bo), (bd_sb, bd)):
                load(dst[:], src.partition_broadcast(P))
            sp.wait_ge(rw_zero, 1)
            for i in range(4):
                for row in (DK * i, P // 2 + DK * i):
                    sp.dma_start(rw_rows[row:row + DK, :, F * i:F * (i + 1)],
                                 rw.rearrange("(b i) k f -> i k b f", i=4)[i]).then_inc(rw_loaded, 16)

            def body(it, par, kv, at, rt, ff, last, batch):
                a, m = it, it - ATTN_LAG
                if kv and not (isinstance(a, int) and a == 0):
                    wait(sp, kv_full, (a - 1) * KV_USES + 2)
                    sp.dma_start(xa[:], x_groups[a]).then_inc(xa_loaded, 16)
                if at:
                    wait(sp, at_read, (m - 1) * AT_USES + AT_U["wo", 1] + 1)
                    sp.dma_start(xb[:], x_groups[m]).then_inc(xb_loaded, 16)

            schedule(sp, body, lambda b: None)

        @block.gpsimd
        def _(pool):
            pool.memset(rw_rows, 0.0).then_inc(rw_zero, 1)
            pool.memset(ident_rows, 0.0).then_inc(pool_prep, 1)
            pool.memset(neg_half[:], -0.5).then_inc(pool_prep, 1)
            pool.memset(kv_blocks[:], 0.0).then_inc(pool_prep, 1)
            pool.memset(v_sb[:, :, :, 2 * DK:VW], 1.0).then_inc(pool_prep, 1)
            pool.wait_ge(pool_prep, 4)
            pool.affine_select(out=ident_rows, in_=ident_rows, compare_op=ALU.not_equal, fill=1.0, base=0,
                               pattern=[[-1, P]], channel_multiplier=1).then_inc(pool_prep, 1)
            pool.wait_ge(pool_prep, 5)
            pool.tensor_copy(ident_r[:], ident_rows).then_inc(pool_prep, 1)
            pool.wait_ge(w_loaded, W_ALL)

            def norm_scale(s_dve, dve_steps, s_own, g, mv, rstd, s_out):
                wait_apart(pool, s_dve, dve_steps)
                pool.tensor_scalar(rstd[:], mv[:, :, 1], LN_EPS, None, ALU.add).then_inc(s_own, 1)
                pool.wait_ge(s_own, g + 1)
                pool.tensor_tensor(rstd[:], rstd[:], neg_half[:], ALU.pow).then_inc(s_out, 1)

            def body(it, par, kv, at, rt, ff, last, batch):
                a, m, s, f = it, it - ATTN_LAG, it - ROUTE_LAG, it - LAST_LAG
                if at:
                    pool.wait_ge(xb_loaded, (m + 1) * 16)
                    pool.wait_ge(at_full, m * AT_USES + 2)
                    pool.tensor_tensor(xb[:], xb[:], bcast(bo_sb[:].unsqueeze(1), [P, T, D]),
                                       ALU.add).then_inc(xb_bias, 1)

                def qp_add(j):
                    wait_apart(pool, at_read, m * AT_USES + AT_U["qp", j] + 1)
                    pool.tensor_scalar(qp[:, j % 4], qp[:, j % 4], ATTN_EPS, 1.0, ALU.add,
                                       ALU.mult).then_inc(qp_eps, 1)

                def kp_add(t):
                    wait_apart(pool, kv_read, a * KV_USES + KV_U["kp", 2 * t + 1] + 1)
                    pool.tensor_scalar(kp[:], kp[:], ATTN_EPS, 1.0, ALU.add,
                                       ALU.mult).then_inc(kp_eps, 1)

                def spread(t, h):
                    if h == 0:
                        pool.wait_ge(rt_exp, s * T + t + 1)
                    wait(pool, rt_dve, s * RT_STEPS + (t - (h < 2)) * len(RT_TILE) + RT_AT["add", (h - 2) % RH])
                    pool.tensor_tensor(grid[:, h % 2], bcast(ex[:, h, 0:NX].unsqueeze(2), [P, NX, NK]),
                                       bcast(ex[:, RH + h, 0:NK].unsqueeze(1), [P, NX, NK]),
                                       ALU.mult).then_inc(spread_ready, 1)

                def adds(uses):
                    for kind, j in uses:
                        if kind == "qp" and at:
                            qp_add(j)
                        if kind == "kp" and kv and j % 2:
                            kp_add(j // 2)

                for c in range(C):
                    t, odd = divmod(c, 2)
                    adds(KV_FIRST[c])
                    adds(AT_EARLY[c])
                    if rt and odd:
                        spread(t, 2)
                    if last and c == 0:
                        norm_scale(y_dve, (f + 1) * Y_STEPS, ln2_pool, f, mv2, rstd2, rstd2_ready)
                    adds(KV_EARLY[c])
                    adds(AT_MID[c])
                    if rt and odd:
                        spread(t, 3)
                    if at and c == 6:
                        norm_scale(at_dve, (m + 1) * AT_STEPS, ln1_pool, m, mv1, rstd1, rstd1_ready)
                    if rt and not odd:
                        spread(t, 0)
                    adds(KV_LATE[c])
                    if last and c == 1:
                        pool.wait_ge(y_ready, (f + 1) * T)
                        pool.dma_start(out_groups[f], y_sb[:]).then_inc(y_stored, 16)
                    if rt and not odd:
                        spread(t, 1)
                    adds(AT_LATE[c])

            schedule(pool, body, lambda b: None)
            pool.wait_ge(y_stored, 16 * NG)

        @block.tensor
        def _(pe):
            pe.wait_ge(w_loaded, W_ALL)
            pe.wait_ge(pool_prep, 6)
            banks = [kv_bank, at_bank]
            for u in range(4):
                if u >= 2:
                    pe.wait_ge(prep_low, u - 1)
                half, quad = divmod(u, 2)
                for j in range(4):
                    c = 4 * quad + j
                    mm = pe.transpose(banks[u % 2][:, j * P:(j + 1) * P],
                                      down_rows[:, c, half * P:(half + 1) * P], ident)
                mm.then_inc(prep_full, 1)
            for u in range(4, 6):
                pe.wait_ge(prep_low, u - 1)
                half = u - 4
                for b in range(4):
                    mm = pe.transpose(banks[u % 2][:, b * P:(b + 1) * P],
                                      wrq_rows[:, half, b * P:(b + 1) * P], ident)
                mm.then_inc(prep_full, 1)
            pe.wait_ge(prep_read, 1)
            for b in range(4):
                mm = pe.transpose(banks[0][:, b * NK:(b + 1) * NK],
                                  keys_rows[:, b // 2, 2 * (b % 2):2 * (b % 2) + 2, :].rearrange("k h n -> k (h n)"),
                                  ident[0:NK, 0:NK])
            mm.then_inc(prep_full, 1)
            pe.wait_ge(prep_read, 3)
            for g2 in range(2):
                r = slice(g2 * RN, (g2 + 1) * RN)
                for half in range(KD):
                    for b in range(4):
                        col = (half * 4 + b) * NK
                        mm = pe.matmul(banks[1 - g2][:, col:col + NK], wrqT[r, b, half * P:(half + 1) * P],
                                       keysT[r, b, :], start=True, stop=True)
                mm.then_inc(prep_full, 1)
            pe.wait_ge(prep_low, 6)
            pe.wait_ge(low_ready, 3)

            def body(it, par, kv, at, rt, ff, last, batch):
                a, m, s, n = it, it - ATTN_LAG, it - ROUTE_LAG, it - FFN_LAG
                other = 1 - par

                def turn(bank, src, half):
                    for t in range(T):
                        mm = pe.transpose(bank[:, t * P:(t + 1) * P], src[:, t, half * P:(half + 1) * P], ident)
                    return mm

                def project(bank, w, srcT, e):
                    for k in range(KD):
                        mm = pe.matmul(bank[:], w[:, k, e * P:(e + 1) * P], srcT[:, k, :],
                                       start=(k == 0), stop=(k == KD - 1))
                    return mm

                def project_rows(bank, srcT, w, t0):
                    for t in (t0, t0 + 1):
                        for k in range(KD):
                            mm = pe.matmul(bank[:, (t - t0) * D:(t - t0 + 1) * D],
                                           srcT[:, k, t * P:(t + 1) * P], w[:, k, :],
                                           start=(k == 0), stop=(k == KD - 1))
                    return mm

                def product(bank, w_hl, wcols, src_hl, scols, swap=False):
                    terms = [(0, 0), (0, 1), (1, 0)]
                    for k in range(KD):
                        for i, (wp, sp) in enumerate(terms):
                            wt, st = w_hl[:, wp, k, wcols], src_hl[:, sp, k, scols]
                            mm = pe.matmul(bank[:], st if swap else wt, wt if swap else st,
                                           start=(k == 0 and i == 0), stop=(k == KD - 1 and i == 2))
                    return mm

                def kv_use(kind, j):
                    wait(pe, kv_read, a * KV_USES + KV_U[kind, j])
                    if kind == "turn":
                        if j == 0:
                            pe.wait_ge(xa_loaded, (a + 1) * 16)
                        mm = turn(kv_bank, xa, j)
                    elif kind == "k":
                        mm = project(kv_bank, wk_sb, xaT, j)
                    elif kind == "v":
                        mm = project_rows(kv_bank, xaT, wv_sb, 2 * j)
                    elif kind == "kp":
                        t, half = divmod(j, 2)
                        for i in range(2):
                            for part in range(2):
                                mm = pe.matmul(kv_bank[:, i * (G // 2):(i + 1) * (G // 2)],
                                               kT_hl[:, 2 * half + i, t * P:(t + 1) * P],
                                               rw_hl[:, part, 2 * half + i, :], start=(part == 0), stop=(part == 1))
                    else:
                        pe.wait_ge(kp_eps, a * T + j + 1)
                        for c in range(FC):
                            mm = pe.matmul(kv_bank[:, c * VW:(c + 1) * VW], kp[:, c * P:(c + 1) * P],
                                           v_sb[:, j % 2, c, :], start=True, stop=True)
                    mm.then_inc(kv_full, 1)

                def at_use(kind, j):
                    wait(pe, at_read, m * AT_USES + AT_U[kind, j])
                    if kind == "turn":
                        if j == 0:
                            pe.wait_ge(xb_loaded, (m + 1) * 16)
                        mm = turn(at_bank, xb, j)
                    elif kind == "q":
                        mm = project(at_bank, wq_sb, xbT, j)
                    elif kind == "qp":
                        for part in range(2):
                            mm = pe.matmul(at_bank[:], rw_hl[:, part, j // 2, (j % 2) * P:(j % 2 + 1) * P],
                                           qT_hl[:, j // 2, :], start=(part == 0), stop=(part == 1))
                    elif kind == "qkv":
                        pe.wait_ge(qp_eps, m * FC + 2 * j + 2)
                        if j == 0:
                            pe.wait_ge(blocks_ready, batch)
                        W = 2 * (DK + 1)
                        for t in range(T):
                            for c in range(2):
                                mm = pe.matmul(at_bank[:, (2 * t + c) * W:(2 * t + c + 1) * W],
                                               qp[:, (2 * j + c) % 4, t * P:(t + 1) * P],
                                               kv_blocks[:, 2 * j + c].rearrange("p a b -> p (a b)"),
                                               start=True, stop=True)
                    elif kind == "back":
                        mm = turn(at_bank, x1, j)
                    elif kind == "wo":
                        mm = project_rows(at_bank, attnT, wo_sb, 2 * j)
                    else:
                        pe.wait_ge(x1_ready, (m + 1) * T)
                        mm = turn(at_bank, x1, j)
                    mm.then_inc(at_full, 1)

                def rt_use(t):
                    if t == 0:
                        pe.wait_ge(at_read, (s + 1) * AT_USES)
                    wait(pe, rt_read, s * T + t)
                    product(rt_bank, route_hl, slice(0, G), x1T_hl[:, other], slice(t * P, (t + 1) * P),
                            swap=True).then_inc(rt_full, 1)

                def hidden(bank, w_hl, c):
                    product(bank, w_hl, slice(c * P, (c + 1) * P), x1T_hl[:, par],
                            slice(0, G)).then_inc(ring_full, 1)

                def ff_gate(c):
                    wait(pe, h_ready, n * C + c)
                    hidden(ring[c % 2], wg_hl, c)

                def ff_up(c):
                    wait(pe, ring_act, (n * C + c) * 2)
                    hidden(ring[1 - c % 2], wu_hl, c)

                def ff_dots(c):
                    pe.wait_ge(ring_act, (n * C + c) * 2 + 1)
                    hidden(ring[c % 2], downT_hl, c)

                def ff_weights(c):
                    wait(pe, wexp_ready, n * C + c)
                    if c == 0:
                        pe.wait_ge(prob_ready, (n + 1) * T)
                    for t in range(T):
                        mm = pe.transpose(pt_bank[:, t * P:(t + 1) * P], prob[:, par, t, c * P:(c + 1) * P],
                                          ident)
                    mm.then_inc(pt_full, 1)

                def ff_out(c, pair):
                    if pair == 0:
                        if c == 0:
                            wait(pe, y_read, n * 2)
                        pe.wait_ge(h_ready, n * C + c + 1)
                        pe.wait_ge(wexp_ready, n * C + c + 1)
                    for t in (2 * pair, 2 * pair + 1):
                        rows = y_bank[pair][:, (t % 2) * D:(t % 2 + 1) * D]
                        if c == C - 2:
                            for k in range(KD):
                                for part in range(2):
                                    pe.matmul(rows[:, k * P:(k + 1) * P],
                                              x1T_hl[:, par, part, k, t * P:(t + 1) * P], ident_r[:],
                                              start=False, stop=False, skip_group_check=True)
                        pe.matmul(rows, gate[:, c % 2, t * P:(t + 1) * P], wd_sb[:, c, :],
                                  start=(c == 0 and t % 2 == 0), stop=False, skip_group_check=True)
                        mm = pe.matmul(rows, wexp[:, c % 2, t * P:(t + 1) * P], up_sb[:, c, :],
                                       start=False, stop=(c == C - 1), skip_group_check=True)
                    if pair == 1:
                        mm.then_inc(y_full, 1)

                for c in range(C):
                    if ff:
                        ff_gate(c)
                    if kv:
                        for use in KV_FIRST[c]:
                            kv_use(*use)
                    if at:
                        for use in AT_EARLY[c]:
                            at_use(*use)
                    if ff:
                        ff_up(c)
                    if rt and c % 2 == 0:
                        rt_use(c // 2)
                    if kv:
                        for use in KV_EARLY[c]:
                            kv_use(*use)
                    if ff:
                        ff_dots(c)
                    if at:
                        for use in AT_MID[c]:
                            at_use(*use)
                    if ff:
                        ff_weights(c)
                        if c:
                            ff_out(c - 1, 0)
                    if kv:
                        for use in KV_LATE[c]:
                            kv_use(*use)
                    if ff and c:
                        ff_out(c - 1, 1)
                    if ff and c == C - 1:
                        ff_out(c, 0)
                    if at:
                        for use in AT_LATE[c][:1]:
                            at_use(*use)
                    if ff and c == C - 1:
                        ff_out(c, 1)
                    if at:
                        for use in AT_LATE[c][1:]:
                            at_use(*use)

            schedule(pe, body, lambda b: None)

        @block.scalar
        def _(act):
            banks = [kv_bank, at_bank]
            for u in range(9):
                act.wait_ge(prep_full, u + 1)
                bank = banks[u % 2]
                if u < 4:
                    half, quad = divmod(u, 2)
                    act.copy(downT_hl[:, 0, half, quad * G:(quad + 1) * G], bank[:]).then_inc(high_ready, 1)
                elif u < 6:
                    act.copy(wrqT[:, :, (u - 4) * P:(u - 3) * P],
                             bank[:].rearrange("p (b d) -> p b d", b=4)).then_inc(prep_read, 1)
                elif u == 6:
                    act.copy(keysT, bank[:, 0:4 * NK].rearrange("p (b k) -> p b k", k=NK)).then_inc(prep_read, 1)
                else:
                    act.copy(route_half(0, u - 7), bank[:].rearrange("p (b n) -> p b n", n=NK)).then_inc(high_ready, 1)
            act.wait_ge(rw_loaded, RW_ALL)
            act.copy(rw_hl[:, 0], rw_rows).then_inc(rw_high, 1)
            act.wait_ge(w_loaded, W_ALL)
            act.copy(wg_hl[:, 0], wg_rows).then_inc(high_ready, 1)
            act.copy(wu_hl[:, 0], wu_rows).then_inc(high_ready, 1)

            def highs(blocks, half, bank, bias, s):
                for i in range(2):
                    rows = slice(i * (P // 2), (i + 1) * (P // 2))
                    ins = act.activation(blocks[rows, 2 * half + i, :], bank[rows], ACT.Identity,
                                         bias=bias[rows, half:half + 1])
                ins.then_inc(s, 1)

            def body(it, par, kv, at, rt, ff, last, batch):
                a, m, s, n = it, it - ATTN_LAG, it - ROUTE_LAG, it - FFN_LAG

                def kv_use(kind, j):
                    if kind in ("v", "sum"):
                        return
                    act.wait_ge(kv_full, a * KV_USES + KV_U[kind, j] + 1)
                    if kind == "turn":
                        ins = act.copy(xaT[:, j, :], kv_bank[:])
                    elif kind == "k":
                        return highs(kT_hl, j, kv_bank, bk_sb, k_high)
                    else:
                        ins = act.activation(kp[:, (j % 2) * G:(j % 2 + 1) * G], kv_bank[:], ACT.Relu)
                    ins.then_inc(kv_read, 1)

                def at_use(kind, j):
                    if kind in ("qkv", "wo"):
                        return
                    act.wait_ge(at_full, m * AT_USES + AT_U[kind, j] + 1)
                    if kind == "turn":
                        act.copy(xbT[:, j, :], at_bank[:]).then_inc(at_read, 1)
                    elif kind == "q":
                        highs(qT_hl, j, at_bank, bq_sb, q_high)
                    elif kind == "qp":
                        act.activation(qp[:, j % 4, :], at_bank[:], ACT.Relu).then_inc(at_read, 1)
                    elif kind == "back":
                        act.copy(attnT[:, j, :], at_bank[:]).then_inc(at_read, 1)
                    else:
                        act.copy(x1T_hl[:, par, 0, j, :], at_bank[:]).then_inc(x1_high, 1)

                def rt_use(t):
                    act.wait_ge(rt_read, s * T + t + 1)
                    act.wait_ge(rt_dve, s * RT_STEPS + t * len(RT_TILE) + RT_AT["less"])
                    act.activation(ex[:], ex[:], ACT.Exp).then_inc(rt_exp, 1)

                def ff_gate(c):
                    act.wait_ge(ring_full, n * (3 * C) + 3 * c + 1)
                    wait(act, y_full, n * C + c - 1)
                    act.activation(gate[:, c % 2], ring[c % 2][:], ACT.Silu,
                                   bias=bg_sb[:, c:c + 1]).then_inc(ring_act, 1)

                def ff_dots(c):
                    act.wait_ge(ring_full, n * (3 * C) + 3 * c + 3)
                    act.activation(wexp[:, c % 2], ring[c % 2][:], ACT.Silu).then_inc(ring_act, 1)

                for c in range(C):
                    if ff:
                        ff_gate(c)
                    if kv:
                        for use in KV_FIRST[c]:
                            kv_use(*use)
                    if at:
                        for use in AT_EARLY[c]:
                            at_use(*use)
                    if kv:
                        for use in KV_EARLY[c]:
                            kv_use(*use)
                    if ff:
                        ff_dots(c)
                    if at:
                        for use in AT_MID[c]:
                            at_use(*use)
                    if rt and c % 2 == 0 and c:
                        rt_use(c // 2)
                    if kv:
                        for use in KV_LATE[c]:
                            kv_use(*use)
                    if at:
                        for use in AT_LATE[c]:
                            at_use(*use)
                    if rt and c == 0:
                        rt_use(0)

            schedule(act, body, lambda b: None)

        @block.vector
        def _(dve):
            dve.memset(kv_sum[:], 0.0).then_inc(sum_cleared, 1)
            banks = [kv_bank, at_bank]

            def low(out, whole, high, s):
                dve.tensor_tensor(out, whole, high.bitcast(F32), ALU.subtract).then_inc(s, 1)

            for u in range(4):
                half, quad = divmod(u, 2)
                cols = slice(quad * G, (quad + 1) * G)
                dve.wait_ge(high_ready, u + 1)
                low(downT_hl[:, 1, half, cols], banks[u % 2][:], downT_hl[:, 0, half, cols], prep_low)
            for g2 in range(2):
                dve.wait_ge(high_ready, 5 + g2)
                low(route_half(1, g2), banks[(7 + g2) % 2][:].rearrange("p (b n) -> p b n", n=NK),
                    route_half(0, g2), prep_low)
            dve.wait_ge(rw_high, 1)
            low(rw_hl[:, 1], rw_rows, rw_hl[:, 0], low_ready)
            dve.wait_ge(w_loaded, W_ALL)
            dve.wait_ge(high_ready, 8)
            low(wg_hl[:, 1], wg_rows, wg_hl[:, 0], low_ready)
            low(wu_hl[:, 1], wu_rows, wu_hl[:, 0], low_ready)
            dve.wait_ge(pool_prep, 6)

            def lows(blocks, half, bank, bias, s):
                for i in range(2):
                    rows, others = (slice(k * (P // 2), (k + 1) * (P // 2)) for k in (i, 1 - i))
                    ins = dve.scalar_tensor_tensor(out=blocks[others, 2 * half + i, :], in0=bank[rows],
                                                   scalar=bias[rows, half:half + 1],
                                                   in1=blocks[rows, 2 * half + i, :].bitcast(F32),
                                                   op0=ALU.add, op1=ALU.subtract)
                ins.then_inc(s, 1)

            def pair(bank):
                return bank[:].rearrange("p (t d) -> p t d", t=2)

            def body(it, par, kv, at, rt, ff, last, batch):
                a, m, s, n, f = it, it - ATTN_LAG, it - ROUTE_LAG, it - FFN_LAG, it - LAST_LAG
                other = 1 - par
                at_steps = Chain(dve, at_dve, m, AT_STEPS)
                rt_steps = Chain(dve, rt_dve, s, RT_STEPS)
                y_steps = Chain(dve, y_dve, f, Y_STEPS)
                marks = {}

                def statistics(rows, stats, mv, steps):
                    for t in range(T):
                        steps.mark(dve.bn_stats(stats[:, t, :], rows[:, t, :]))
                    steps.wait_apart()
                    for t in range(T):
                        steps.mark(dve.bn_aggr(mv[:, t, :], stats[:, t, :]))

                def kv_use(kind, j):
                    if kind == "k":
                        dve.wait_ge(k_high, a * KD + j + 1)
                        lows(kT_hl, j, kv_bank, bk_sb, kv_read)
                    elif kind == "v":
                        dve.wait_ge(kv_full, a * KV_USES + KV_U[kind, j] + 1)
                        dve.tensor_tensor(v_sb[:, :, :, 0:2 * DK],
                                          kv_bank[:].rearrange("p (t c w) -> p t c w", t=2, c=FC),
                                          bcast(bv_sb[:].rearrange("p (c w) -> p c w", c=FC).unsqueeze(1),
                                                [P, 2, FC, 2 * DK]), ALU.add).then_inc(kv_read, 1)
                    elif kind == "sum":
                        dve.wait_ge(kv_full, a * KV_USES + KV_U[kind, j] + 1)
                        dve.wait_ge(sum_cleared, batch + 1)
                        dve.tensor_tensor(kv_sum[:], kv_bank[:, 0:FC * VW].rearrange("p (c w) -> p c w", c=FC),
                                          kv_sum[:], ALU.add).then_inc(kv_read, 1)

                def at_use(kind, j):
                    if kind == "q":
                        dve.wait_ge(q_high, m * KD + j + 1)
                        lows(qT_hl, j, at_bank, bq_sb, at_read)
                    elif kind == "qkv":
                        heads = at_bank[:, 0:4 * T * (DK + 1)].rearrange("p (t h w) -> p t h w", t=T, h=4)
                        rows = x1[:].rearrange("p t (i h w) -> p t i h w", i=4, h=4)[:, :, j]
                        if j == 0 and last:
                            dve.wait_ge(y_stored, (f + 1) * 16)
                        dve.wait_ge(at_full, m * AT_USES + AT_U[kind, j] + 1)
                        at_steps.mark(dve.tensor_scalar(den[:], heads[:, :, :, DK], ATTN_EPS, None, ALU.add))
                        at_steps.wait()
                        at_steps.mark(dve.reciprocal(den[:], den[:]))
                        at_steps.wait()
                        dve.tensor_tensor(rows, heads[:, :, :, 0:DK],
                                          bcast(den[:].unsqueeze(3), [P, T, 4, DK]),
                                          ALU.mult).then_inc(at_read, 1)
                    elif kind == "wo":
                        if j == 0:
                            dve.wait_ge(xb_bias, m + 1)
                        dve.wait_ge(at_full, m * AT_USES + AT_U[kind, j] + 1)
                        dve.tensor_tensor(x1[:, 2 * j:2 * j + 2, :], pair(at_bank), xb[:, 2 * j:2 * j + 2, :],
                                          ALU.add).then_inc(at_read, 1)
                    elif kind == "next":
                        dve.wait_ge(x1_high, m * 2 + j + 1)
                        low(x1T_hl[:, par, 1, j, :], at_bank[:], x1T_hl[:, par, 0, j, :], at_read)

                def norm1_stats():
                    dve.wait_ge(at_read, m * AT_USES + AT_U["wo", 1] + 1)
                    statistics(x1, stats, mv1, at_steps)

                def norm1():
                    dve.wait_ge(rstd1_ready, m + 1)
                    for t in range(T):
                        dve.tensor_scalar(x1[:, t, :], x1[:, t, :], mv1[:, t, 0:1], rstd1[:, t:t + 1],
                                          ALU.subtract, ALU.mult).then_inc(x1_ready, 1)

                def scores(t):
                    rt_steps.wait()
                    wait_apart(dve, rt_full, s * T + t + 1)
                    for g in range(2 * RH):
                        ins = dve.max(top[:, g, :], rt_bank[:, g * NK:(g + 1) * NK])
                    rt_steps.mark(ins)
                    rt_steps.wait()
                    dve.tensor_tensor(ex[:, :, 0:NK], rt_bank[:].rearrange("p (g k) -> p g k", k=NK),
                                      bcast(top[:, :, 0:1], [P, 2 * RH, NK]), ALU.subtract).then_inc(rt_read, 1)
                    rt_steps.mark(dve.tensor_tensor(ex[:, :, NK:], top[:], bcast(top[:, :, 0:1], [P, 2 * RH, TOP]),
                                                    ALU.subtract))

                def choose(t):
                    dve.wait_ge(rt_exp, s * T + t + 1)
                    rt_steps.mark(dve.tensor_tensor(
                        cand[:], bcast(ex[:, 0:RH, NK:].unsqueeze(3), [P, RH, TOP, TOP]),
                        bcast(ex[:, RH:, NK:].unsqueeze(2), [P, RH, TOP, TOP]), ALU.mult))
                    rt_steps.wait_apart()
                    for h in range(RH):
                        ins = dve.max(best[:, h, :], cand[:, h].rearrange("p a b -> p (a b)"))
                    rt_steps.mark(ins)
                    rt_steps.wait()
                    rt_steps.mark(dve.reduce_sum(zsum[:], best[:], AX.X))
                    rt_steps.wait()
                    marks["rz"] = rt_steps.mark(dve.reciprocal(rz[:], zsum[:]))

                def keep(t, h):
                    dve.wait_ge(spread_ready, s * (RH * T) + t * RH + h + 1)
                    g = grid[:, h % 2].rearrange("p a b -> p (a b)")
                    marks["keep", h] = rt_steps.mark(dve.scalar_tensor_tensor(
                        out=g, in0=g, scalar=best[:, h, TOP - 1:TOP], in1=g, op0=ALU.is_ge, op1=ALU.mult))

                def add_head(t, h):
                    g = grid[:, h % 2].rearrange("p a b -> p (a b)")
                    row = prob[:, other, t, :]
                    rt_steps.wait(marks["keep", h])
                    if h == 0:
                        rt_steps.wait(max(marks["rz"], marks["keep", h]))
                        if t == 0:
                            wait(dve, pt_full, (s - 1) * C)
                        ins = dve.tensor_scalar(row, g, rz[:, 0:1], None, ALU.mult)
                    else:
                        rt_steps.wait(marks["add", h - 1])
                        ins = dve.scalar_tensor_tensor(out=row, in0=g, scalar=rz[:, h:h + 1], in1=row,
                                                       op0=ALU.mult, op1=ALU.add,
                                                       accum_out=mass[:, 0:1] if h == RH - 1 else None)
                    marks["add", h] = rt_steps.mark(ins)

                def clamp(t):
                    rt_steps.wait()
                    rt_steps.mark(dve.tensor_scalar(mass[:, 1:2], mass[:, 0:1], -1.0, float(RH), ALU.mult, ALU.add))
                    rt_steps.wait()
                    last = prob[:, other, t, NEXP - 1:NEXP]
                    dve.tensor_tensor(last, last, mass[:, 1:2], ALU.add).then_inc(prob_ready, 1)

                def ff_h(c):
                    dve.wait_ge(ring_full, n * (3 * C) + 3 * c + 2)
                    dve.wait_ge(ring_act, n * (2 * C) + 2 * c + 1)
                    dve.scalar_tensor_tensor(out=gate[:, c % 2], in0=ring[1 - c % 2][:], scalar=bu_sb[:, c:c + 1],
                                             in1=gate[:, c % 2], op0=ALU.add, op1=ALU.mult).then_inc(h_ready, 1)

                def ff_wexp(c):
                    dve.wait_ge(pt_full, n * C + c + 1)
                    dve.wait_ge(ring_act, n * (2 * C) + 2 * c + 2)
                    dve.tensor_tensor(wexp[:, c % 2], pt_bank[:], wexp[:, c % 2], ALU.mult).then_inc(wexp_ready, 1)

                def y_rows():
                    dve.wait_ge(y_full, (f + 1) * C)
                    dve.wait_ge(at_full, (min(m, NG) if isinstance(m, int) else m) * AT_USES)
                    wait(dve, y_stored, f * 16)
                    for i in range(2):
                        dve.tensor_tensor(y_sb[:, 2 * i:2 * i + 2, :], pair(y_bank[i]),
                                          bcast(bd_sb[:].unsqueeze(1), [P, 2, D]), ALU.add).then_inc(y_read, 1)
                    dve.wait_ge(y_read, (f + 1) * 2)
                    statistics(y_sb, stats, mv2, y_steps)

                def norm2():
                    dve.wait_ge(rstd2_ready, f + 1)
                    for t in range(T):
                        dve.tensor_scalar(y_sb[:, t, :], y_sb[:, t, :], mv2[:, t, 0:1], rstd2[:, t:t + 1],
                                          ALU.subtract, ALU.mult).then_inc(y_ready, 1)

                def uses(kinds):
                    for use in kinds:
                        if use[0] in ("k", "v", "sum") and kv:
                            kv_use(*use)
                        if use[0] in ("q", "qkv", "wo", "next") and at:
                            at_use(*use)

                for c in range(C):
                    t, odd = divmod(c, 2)
                    if last and c == 0:
                        y_rows()
                    uses(KV_FIRST[c])
                    uses(AT_EARLY[c])
                    if rt and odd:
                        keep(t, 1), add_head(t, 0)
                    if ff:
                        ff_h(c)
                    if rt and not odd:
                        scores(t)
                    uses(KV_EARLY[c])
                    if rt and odd:
                        keep(t, 2), add_head(t, 1)
                    uses(AT_MID[c])
                    if at and c == 6:
                        norm1_stats()
                    if ff:
                        ff_wexp(c)
                    if rt and odd:
                        keep(t, 3)
                    uses(KV_LATE[c])
                    if at and c == 7:
                        norm1()
                    if rt and odd:
                        add_head(t, 2)
                    if rt and not odd and c:
                        choose(t)
                    uses(AT_LATE[c])
                    if last and c == 0:
                        norm2()
                    if rt and c == 0:
                        choose(0)
                    if rt and odd:
                        add_head(t, 3), clamp(t)
                    if rt and not odd:
                        keep(t, 0)
                assert not rt or rt_steps.k == RT_STEPS
                assert not at or at_steps.k == AT_STEPS

            def batch_end(b):
                dve.wait_ge(kv_read, (b + 1) * (BG * KV_USES))
                for g2 in range(2):
                    rows = slice(g2 * F, (g2 + 1) * F)
                    dve.tensor_copy(kv_blocks[rows, :, g2, 0:DK], kv_sum[rows, :, g2 * DK:(g2 + 1) * DK])
                    ins = dve.tensor_copy(kv_blocks[rows, :, g2, DK:DK + 1], kv_sum[rows, :, 2 * DK:VW])
                ins.then_inc(blocks_ready, 1)
                dve.wait_ge(blocks_ready, b + 1)
                dve.memset(kv_sum[:], 0.0).then_inc(sum_cleared, 1)

            schedule(dve, body, batch_end)


_INS = ["x", "Wq", "bq", "Wk", "bk", "Wv", "bv", "Wo", "bo", "rw"]
_FFN = ["Wg", "bg", "Wu", "bu", "Wd", "bd", "Wq", "keys", "down_embed", "up_embed"]


def kernel(**inputs):
    import numpy as _np
    import concourse.bacc as _bacc
    from concourse import mybir as _mybir
    from concourse.bass_utils import run_bass_kernel_spmd as _run

    nc = _bacc.Bacc("TRN2", target_bir_lowering=False, num_devices=1)
    arrays, args = {}, []
    for name in [f"L0_attn_{n}" for n in _INS] + [f"L0_ffn_{n}" for n in _FFN]:
        a = _np.ascontiguousarray(inputs[name])
        arrays[f"in_{name}"] = a
        args.append(nc.dram_tensor(f"in_{name}", a.shape, _mybir.dt.from_np(a.dtype), kind="ExternalInput").ap())
    shape = inputs["L0_attn_x"].shape
    args.append(nc.dram_tensor("out_y", shape, _mybir.dt.float32, kind="ExternalOutput").ap())
    block_kernel(nc, *args)
    r = _run(nc, [arrays], core_ids=[0])
    return r.results[0]["out_y"]
```

```python
from contextlib import ExitStack

import concourse.bass as bass
from concourse import mybir

F32 = mybir.dt.float32
F32R = mybir.dt.float32r
ALU = mybir.AluOpType
ACT = mybir.ActivationFunctionType
AX = mybir.AxisListType

P = 128


def block_kernel(nc, x, Wq, bq, Wk, bk, Wv, bv, Wo, bo, rw, Wg, bg, Wu, bu, Wd, bd,
                 Wrq, keys, down, up, out):
    B, S, D = x.shape
    H, DK, F = rw.shape
    KD = D // P
    HF = H * F
    FC = HF // P
    VW = 2 * DK + 1
    DFF = Wg.shape[1]
    NEXP = down.shape[0]
    C = DFF // P
    RH, NK, _, RN = keys.shape
    TOP = 8
    NX = NEXP // NK
    T = 4
    G = T * P
    NG = B * S // G
    BG = S // G
    ATTN_EPS, LN_EPS = 1e-6, 1e-5
    assert KD == 2 and FC == 8 and C == 8 and NEXP == DFF and BG == 4 and NG % 2 == 0

    ATTN_LAG, ROUTE_LAG, FFN_LAG, LAST_LAG = BG, BG + 1, BG + 2, BG + 3

    KV_TILE = [[("kp", 2 * t), ("kp", 2 * t + 1), ("sum", t)] for t in range(T)]
    KV_SEQ = ([("turn", 0), ("turn", 1), ("k", 0), ("k", 1), ("v", 0)] + KV_TILE[0] + KV_TILE[1]
              + [("v", 1)] + KV_TILE[2] + KV_TILE[3])
    AT_SEQ = ([("turn", 0), ("turn", 1), ("q", 0), ("q", 1)] + [("qp", j) for j in range(4)] + [("qkv", 0)]
              + [("qp", 4), ("qp", 5), ("qkv", 1), ("qp", 6), ("qp", 7), ("qkv", 2), ("qkv", 3)]
              + [("back", 0), ("back", 1), ("wo", 0), ("wo", 1), ("next", 0), ("next", 1)])
    KV_USES, AT_USES = len(KV_SEQ), len(AT_SEQ)
    KV_U = {use: u for u, use in enumerate(KV_SEQ)}
    AT_U = {use: u for u, use in enumerate(AT_SEQ)}

    x_groups = x.rearrange("b s d -> (b s) d").rearrange("(g p t) d -> g p t d", p=P, t=T)
    out_groups = out.rearrange("b s d -> (b s) d").rearrange("(g p t) d -> g p t d", p=P, t=T)

    with ExitStack() as ctx:
        def sb(name, *shape, dt=F32):
            return ctx.enter_context(nc.sbuf_tensor(name, list(shape), dt))

        def ps(name):
            return ctx.enter_context(nc.psum_tensor(name, [P, G], F32))

        def sem(name):
            return ctx.enter_context(nc.semaphore(name))

        wq_sb, wk_sb, wv_sb, wo_sb = (sb(n, P, KD, D) for n in ("wq_sb", "wk_sb", "wv_sb", "wo_sb"))
        rw_hl = sb("rw_hl", P, 2, 2 * KD, G // 2, dt=F32R)
        wg_hl, wu_hl, downT_hl = (sb(n, P, 2, KD, DFF, dt=F32R) for n in ("wg_hl", "wu_hl", "downT_hl"))
        route_hl = sb("route_hl", P, 2, KD, G, dt=F32R)
        ident_r = sb("ident_r", P, P, dt=F32R)
        ident = ident_r[:].bitcast(F32)
        wd_sb, up_sb = sb("wd_sb", P, C, D), sb("up_sb", P, C, D)
        bq_sb, bk_sb = sb("bq_sb", P, KD), sb("bk_sb", P, KD)
        bg_sb, bu_sb = sb("bg_sb", P, C), sb("bu_sb", P, C)
        bv_sb, bo_sb, bd_sb = (sb(n, P, D) for n in ("bv_sb", "bo_sb", "bd_sb"))
        neg_half = sb("neg_half", P, T)
        xa = sb("xa", P, T, D)
        xaT = sb("xaT", P, KD, G)
        kT_hl = sb("kT_hl", P, 2 * KD, G, dt=F32R)
        kp = sb("kp", P, HF)
        v_sb = sb("v_sb", P, 2, FC, VW)
        kv_sum = sb("kv_sum", P, FC, VW)
        kv_blocks = sb("kv_blocks", P, FC, 2, DK + 1)
        xb = sb("xb", P, T, D)
        qT_hl = sb("qT_hl", P, 2 * KD, G, dt=F32R)
        qp = sb("qp", P, 4, G)
        xbT = qp[:, 2:4]
        den = sb("den", P, T, 4)
        attnT = xbT
        x1 = sb("x1", P, T, D)
        stats, mv1, rstd1 = sb("stats", P, T, 6), sb("mv1", P, T, 2), sb("rstd1", P, T)
        x1T_hl = sb("x1T_hl", P, 2, 2, KD, G, dt=F32R)
        top = sb("top", P, 2 * RH, TOP)
        ex = sb("ex", P, 2 * RH, NK + TOP)
        cand = sb("cand", P, RH, TOP, TOP)
        best = sb("best", P, RH, TOP)
        zsum, rz = sb("zsum", P, RH), sb("rz", P, RH)
        grid = sb("grid", P, 2, NX, NK)
        prob = sb("prob", P, 2, T, NEXP)
        mass = sb("mass", P, 2)
        gate = sb("gate", P, 2, G)
        wexp = sb("wexp", P, 2, G)
        y_sb = x1
        mv2, rstd2 = sb("mv2", P, T, 2), sb("rstd2", P, T)

        kp2 = qp[:, 0:2].rearrange("p a n -> p (a n)")
        v2_sb = gate[:].rearrange("p a n -> p (a n)")[:, 0:2 * FC * VW].rearrange("p (t c w) -> p t c w", t=2, c=FC)

        kv_bank, at_bank, rt_bank = ps("kv_bank"), ps("at_bank"), ps("rt_bank")
        pt_bank = ps("pt_bank")
        ring = [ps("ring0"), ps("ring1")]
        y_bank = [ps("y_bank0"), ps("y_bank1")]

        kvw_loaded, w_loaded = sem("kvw_loaded"), sem("w_loaded")
        rw_zero, rw_loaded = sem("rw_zero"), sem("rw_loaded")
        pool_prep, prep_full, prep_read = sem("pool_prep"), sem("prep_full"), sem("prep_read")
        high_ready, low_ready, prep_low = sem("high_ready"), sem("low_ready"), sem("prep_low")
        rw_high = sem("rw_high")
        xa_loaded = sem("xa_loaded")
        kv_full, kv_read = sem("kv_full"), sem("kv_read")
        k_high, kp_eps = sem("k_high"), sem("kp_eps")
        blocks_ready, sum_cleared = sem("blocks_ready"), sem("sum_cleared")
        xa2_loaded, kv2_full, kv2_read = sem("xa2_loaded"), sem("kv2_full"), sem("kv2_read")
        k2_high, kp2_eps = sem("k2_high"), sem("kp2_eps")
        xb_loaded, xb_bias, x1_high = sem("xb_loaded"), sem("xb_bias"), sem("x1_high")
        at_full, at_read = sem("at_full"), sem("at_read")
        q_high, qp_eps = sem("q_high"), sem("qp_eps")
        at_dve, rstd1_ready, x1_ready = sem("at_dve"), sem("rstd1_ready"), sem("x1_ready")
        ln1_pool = sem("ln1_pool")
        rt_full, rt_read, rt_exp, rt_dve = sem("rt_full"), sem("rt_read"), sem("rt_exp"), sem("rt_dve")
        spread_ready, prob_ready = sem("spread_ready"), sem("prob_ready")
        ring_full, ring_act = sem("ring_full"), sem("ring_act")
        pt_full, h_ready, wexp_ready = sem("pt_full"), sem("h_ready"), sem("wexp_ready")
        y_full, y_read, y_dve = sem("y_full"), sem("y_read"), sem("y_dve")
        ln2_pool, rstd2_ready, y_ready, y_stored = (sem("ln2_pool"), sem("rstd2_ready"),
                                                    sem("y_ready"), sem("y_stored"))

        AT_STEPS = 2 * T + 2 * T
        RT_TILE = (["top", "less", "cand", "best", "sum", "rz"]
                   + [(step, h) for h in range(RH) for step in ("keep", "add")] + ["mass"])
        RT_AT = {name: k + 1 for k, name in enumerate(RT_TILE)}
        RT_STEPS = len(RT_TILE) * T
        Y_STEPS = 2 * T

        AT_EARLY = [AT_SEQ[3 * c:3 * c + 1] for c in range(7)] + [[]]
        AT_MID = [AT_SEQ[3 * c + 1:3 * c + 2] if c < 6 else [] for c in range(7)] + [[]]
        AT_LATE = [AT_SEQ[3 * c + 2:3 * c + 3] for c in range(6)] + [[], AT_SEQ[-2:]]
        AT_MID[6] = [("wo", 1)]
        kv_places = [(c, place) for c in range(C) for place in range(3) if place or c >= C - 2]
        kv_place = {at: [use] for at, use in zip(kv_places, KV_SEQ)}
        KV_FIRST, KV_EARLY, KV_LATE = ([kv_place.get((c, place), []) for c in range(C)] for place in range(3))
        assert len(kv_places) == KV_USES

        stage = prob[:].rearrange("p a t e -> p (a t e)")
        cut = lambda at, n: stage[:, at:at + n]
        down_rows = cut(0, C * D).rearrange("p (c d) -> p c d", d=D)
        wg_rows = cut(C * D, KD * DFF).rearrange("p (k n) -> p k n", k=KD)
        wu_rows = cut(C * D + KD * DFF, KD * DFF).rearrange("p (k n) -> p k n", k=KD)
        wrq_rows = cut(C * D + 2 * KD * DFF, KD * G).rearrange("p (k n) -> p k n", k=KD)
        keys_rows = cut(C * D + 2 * KD * DFF + KD * G, 2 * RH * RN)[0:NK].rearrange("k (a h n) -> k a h n", h=RH, a=2)
        wrqT = x1[:]
        stage2 = grid[:].rearrange("p g a b -> p (g a b)")
        rw_rows = stage2[:, 0:KD * G].rearrange("p (b n) -> p b n", b=2 * KD)
        ident_rows = stage2[:, KD * G:KD * G + P]
        keysT = stage2[:, KD * G + P:KD * G + P + 4 * NK].rearrange("p (b k) -> p b k", k=NK)

        def route_half(part, g2):
            return route_hl[:, part].rearrange("p k (b g n) -> p (k b) g n", b=4, g=2)[:, :, g2, :]

        block = ctx.enter_context(nc.Block())

        def wait(eng, s, value):
            if not (isinstance(value, int) and value <= 0):
                eng.wait_ge(s, value)

        def wait_apart(eng, *waits):
            waits = [(s, value if isinstance(value, int) else eng.to_reg(value)) for s, value in waits]
            eng.wait_ge(pool_prep, 5)
            for s, value in waits:
                wait(eng, s, value)

        class Lane:

            def __init__(self, bank, x, xT, k_hl, kp, v, loaded, full, read, high, eps):
                self.bank, self.x, self.xT, self.k_hl, self.kp, self.v = bank, x, xT, k_hl, kp, v
                self.loaded, self.full, self.read, self.high, self.eps = loaded, full, read, high, eps

        LANES = [Lane(kv_bank, xa, xaT, kT_hl, kp, v_sb, xa_loaded, kv_full, kv_read, k_high, kp_eps),
                 Lane(at_bank, xb, xbT, qT_hl, kp2, v2_sb, xa2_loaded, kv2_full, kv2_read, k2_high, kp2_eps)]
        main, second = LANES
        FILL = BG // 2

        def in_main(a):
            return a - FILL

        def fill_lanes(use, prep):
            for r in range(FILL):
                for k, (kind, j) in enumerate(KV_SEQ):
                    for lane in LANES:
                        use(lane, r, kind, j)
                    if r == FILL - 1 and k < PREP_STEPS:
                        prep(k)

        class Chain:

            def __init__(self, eng, s, group, steps):
                self.eng, self.s, self.base, self.steps, self.k = eng, s, group * steps, steps, 0

            def mark(self, ins):
                self.k += 1
                assert self.k <= self.steps
                ins.then_inc(self.s, 1)

                return self.k

            def wait(self, k=None):
                wait(self.eng, self.s, self.base + (k or self.k))

            def wait_apart(self):
                wait_apart(self.eng, (self.s, self.base + self.k))

        def bcast(ap, shape):
            return ap.broadcast_to(shape)

        def schedule(eng, body, batch_end):
            def step(it, par, batch=None):
                live = lambda lag: not isinstance(it, int) or 0 <= it - lag < NG
                body(it, par, live(0), live(ATTN_LAG), live(ROUTE_LAG), live(FFN_LAG), live(LAST_LAG), batch)

            batch_end(0)
            for it in range(BG, 2 * BG):
                step(it, it % 2, it // BG)
            batch_end(1)
            with eng.Fori(2, B) as b:
                with eng.Fori(0, BG // 2) as j:
                    for par in range(2):
                        step(b * BG + j * 2 + par, par, b)
                batch_end(b)
            with eng.Fori(0, BG // 2) as j:
                for par in range(2):
                    it = j * 2 + (NG + par)
                    body(it, par, False, True, True, True, True, B)
            for it in range(NG + BG, NG + LAST_LAG):
                step(it, it % 2, it // BG)

        PREP_STEPS, PREP_WG, PREP_WU = 11, 9, 10
        KVW_ALL = 16 * 4
        W_ALL = 16 * (4 + 4 + 2 + 3 + 2)
        RW_ALL = 16 * 8

        @block.sync
        def _(sp):
            def load(dst, src, done=w_loaded, by_element=False):
                sp.dma_start(dst, src, allow_slow_non_contiguous=by_element).then_inc(done, 16)

            sp.dma_start(xa[:], x_groups[0]).then_inc(xa_loaded, 16)
            load(wk_sb[:], Wk.rearrange("(c p) n -> p c n", p=P), kvw_loaded)
            load(bk_sb[:], bk.rearrange("(c p) -> p c", p=P), kvw_loaded, by_element=True)
            load(wv_sb[:], Wv.rearrange("(c p) n -> p c n", p=P), kvw_loaded)
            load(bv_sb[:], bv.partition_broadcast(P), kvw_loaded)
            sp.dma_start(xb[:], x_groups[1]).then_inc(xa2_loaded, 16)
            sp.wait_ge(rw_zero, 1)
            for i in range(4):
                for row in (DK * i, P // 2 + DK * i):
                    sp.dma_start(rw_rows[row:row + DK, :, F * i:F * (i + 1)],
                                 rw.rearrange("(b i) k f -> i k b f", i=4)[i]).then_inc(rw_loaded, 16)
            for dst, src in ((down_rows, down), (wrq_rows, Wrq), (wg_rows, Wg), (wu_rows, Wu)):
                load(dst, src.rearrange("(c p) n -> p c n", p=P))
            for half in range(2):
                load(keys_rows[:, half], keys[:, :, half, :].rearrange("h k n -> k h n"))
            for dst, src in ((wq_sb, Wq), (wo_sb, Wo), (wd_sb, Wd), (up_sb, up)):
                load(dst[:], src.rearrange("(c p) n -> p c n", p=P))
            for dst, src in ((bq_sb, bq), (bg_sb, bg), (bu_sb, bu)):
                load(dst[:], src.rearrange("(c p) -> p c", p=P), by_element=True)
            for dst, src in ((bo_sb, bo), (bd_sb, bd)):
                load(dst[:], src.partition_broadcast(P))
            for r in range(1, FILL):
                for k, lane in enumerate(LANES):
                    sp.wait_ge(lane.full, (r - 1) * KV_USES + 2)
                    sp.dma_start(lane.x[:], x_groups[2 * r + k]).then_inc(lane.loaded, 16)

            def body(it, par, kv, at, rt, ff, last, batch):
                a, m = it, it - ATTN_LAG
                if kv:
                    wait(sp, kv_full, (in_main(a) - 1) * KV_USES + 2)
                    sp.dma_start(xa[:], x_groups[a]).then_inc(xa_loaded, 16)
                if at:
                    if isinstance(m, int) and m == 0:
                        sp.wait_ge(kv2_full, (FILL - 1) * KV_USES + 2)
                    wait(sp, at_read, (m - 1) * AT_USES + AT_U["wo", 1] + 1)
                    sp.dma_start(xb[:], x_groups[m]).then_inc(xb_loaded, 16)

            schedule(sp, body, lambda b: None)

        @block.gpsimd
        def _(pool):
            pool.memset(rw_rows, 0.0).then_inc(rw_zero, 1)
            pool.memset(ident_rows, 0.0).then_inc(pool_prep, 1)
            pool.memset(neg_half[:], -0.5).then_inc(pool_prep, 1)
            pool.memset(kv_blocks[:], 0.0).then_inc(pool_prep, 1)
            pool.memset(v_sb[:, :, :, 2 * DK:VW], 1.0).then_inc(pool_prep, 1)
            pool.memset(v2_sb[:, :, :, 2 * DK:VW], 1.0).then_inc(pool_prep, 1)
            pool.wait_ge(pool_prep, 5)
            pool.affine_select(out=ident_rows, in_=ident_rows, compare_op=ALU.not_equal, fill=1.0, base=0,
                               pattern=[[-1, P]], channel_multiplier=1).then_inc(pool_prep, 1)
            pool.wait_ge(pool_prep, 6)
            pool.tensor_copy(ident_r[:], ident_rows).then_inc(pool_prep, 1)

            def kv_use(lane, i, kind, j):
                if kind == "kp" and j % 2:
                    wait_apart(pool, (lane.read, i * KV_USES + KV_U["kp", j] + 1))
                    pool.tensor_scalar(lane.kp[:], lane.kp[:], ATTN_EPS, 1.0, ALU.add, ALU.mult).then_inc(lane.eps, 1)

            fill_lanes(kv_use, lambda k: None)
            pool.wait_ge(w_loaded, W_ALL)

            def norm_scale(s_dve, dve_steps, s_own, g, mv, rstd, s_out):
                wait_apart(pool, (s_dve, dve_steps))
                pool.tensor_scalar(rstd[:], mv[:, :, 1], LN_EPS, None, ALU.add).then_inc(s_own, 1)
                pool.wait_ge(s_own, g + 1)
                pool.tensor_tensor(rstd[:], rstd[:], neg_half[:], ALU.pow).then_inc(s_out, 1)

            def body(it, par, kv, at, rt, ff, last, batch):
                a, m, s, f = it, it - ATTN_LAG, it - ROUTE_LAG, it - LAST_LAG
                if at:
                    pool.wait_ge(xb_loaded, (m + 1) * 16)
                    pool.wait_ge(at_full, m * AT_USES + 2)
                    pool.tensor_tensor(xb[:], xb[:], bcast(bo_sb[:].unsqueeze(1), [P, T, D]),
                                       ALU.add).then_inc(xb_bias, 1)

                def qp_add(j):
                    wait_apart(pool, (at_read, m * AT_USES + AT_U["qp", j] + 1))
                    pool.tensor_scalar(qp[:, j % 4], qp[:, j % 4], ATTN_EPS, 1.0, ALU.add,
                                       ALU.mult).then_inc(qp_eps, 1)

                def spread(t, h):
                    if h == 0:
                        pool.wait_ge(rt_exp, s * T + t + 1)
                    wait(pool, rt_dve, s * RT_STEPS + (t - (h < 2)) * len(RT_TILE) + RT_AT["add", (h - 2) % RH])
                    pool.tensor_tensor(grid[:, h % 2], bcast(ex[:, h, 0:NX].unsqueeze(2), [P, NX, NK]),
                                       bcast(ex[:, RH + h, 0:NK].unsqueeze(1), [P, NX, NK]),
                                       ALU.mult).then_inc(spread_ready, 1)

                def adds(uses):
                    for kind, j in uses:
                        if kind == "qp" and at:
                            qp_add(j)
                        if kind == "kp" and kv:
                            kv_use(main, in_main(a), kind, j)

                for c in range(C):
                    t, odd = divmod(c, 2)
                    adds(KV_FIRST[c])
                    adds(AT_EARLY[c])
                    if rt and odd:
                        spread(t, 2)
                    if last and c == 0:
                        norm_scale(y_dve, (f + 1) * Y_STEPS, ln2_pool, f, mv2, rstd2, rstd2_ready)
                    adds(KV_EARLY[c])
                    adds(AT_MID[c])
                    if rt and odd:
                        spread(t, 3)
                    if at and c == 6:
                        norm_scale(at_dve, (m + 1) * AT_STEPS, ln1_pool, m, mv1, rstd1, rstd1_ready)
                    if rt and not odd:
                        spread(t, 0)
                    adds(KV_LATE[c])
                    if last and c == 1:
                        pool.wait_ge(y_ready, (f + 1) * T)
                        pool.dma_start(out_groups[f], y_sb[:]).then_inc(y_stored, 16)
                    if rt and not odd:
                        spread(t, 1)
                    adds(AT_LATE[c])

            schedule(pool, body, lambda b: None)
            pool.wait_ge(y_stored, 16 * NG)

        @block.tensor
        def _(pe):
            banks = ring

            def prep(k):
                bank = banks[k % 2]
                if k == 0:
                    pe.wait_ge(w_loaded, W_ALL)
                if k < 4:
                    if k >= 2:
                        pe.wait_ge(prep_low, k - 1)
                    half, quad = divmod(k, 2)
                    for b in range(4):
                        mm = pe.transpose(bank[:, b * P:(b + 1) * P],
                                          down_rows[:, 4 * quad + b, half * P:(half + 1) * P], ident)
                elif k < 6:
                    pe.wait_ge(prep_low, k - 1)
                    for b in range(4):
                        mm = pe.transpose(bank[:, b * P:(b + 1) * P], wrq_rows[:, k - 4, b * P:(b + 1) * P], ident)
                elif k == 6:
                    pe.wait_ge(prep_read, 1)
                    for b in range(4):
                        mm = pe.transpose(bank[:, b * NK:(b + 1) * NK],
                                          keys_rows[:, b // 2, 2 * (b % 2):2 * (b % 2) + 2, :].rearrange("k h n -> k (h n)"),
                                          ident[0:NK, 0:NK])
                elif k < 9:
                    g2 = k - 7
                    pe.wait_ge(prep_read, 3)
                    r = slice(g2 * RN, (g2 + 1) * RN)
                    for half in range(KD):
                        for b in range(4):
                            col = (half * 4 + b) * NK
                            mm = pe.matmul(bank[:, col:col + NK], wrqT[r, b, half * P:(half + 1) * P],
                                           keysT[r, b, :], start=True, stop=True)
                else:
                    return
                mm.then_inc(prep_full, 1)

            def turn(bank, src, half):
                for t in range(T):
                    mm = pe.transpose(bank[:, t * P:(t + 1) * P], src[:, t, half * P:(half + 1) * P], ident)
                return mm

            def project(bank, w, srcT, e):
                for k in range(KD):
                    mm = pe.matmul(bank[:], w[:, k, e * P:(e + 1) * P], srcT[:, k, :],
                                   start=(k == 0), stop=(k == KD - 1))
                return mm

            def project_rows(bank, srcT, w, t0):
                for t in (t0, t0 + 1):
                    for k in range(KD):
                        mm = pe.matmul(bank[:, (t - t0) * D:(t - t0 + 1) * D],
                                       srcT[:, k, t * P:(t + 1) * P], w[:, k, :],
                                       start=(k == 0), stop=(k == KD - 1))
                return mm

            def kv_use(lane, i, kind, j):
                bank = lane.bank
                wait(pe, lane.read, i * KV_USES + KV_U[kind, j])
                if kind == "turn":
                    if j == 0:
                        pe.wait_ge(lane.loaded, (i + 1) * 16)
                    mm = turn(bank, lane.x, j)
                elif kind == "k":
                    if lane is main and isinstance(i, int) and i == j == 0:
                        pe.wait_ge(kvw_loaded, KVW_ALL)
                    mm = project(bank, wk_sb, lane.xT, j)
                elif kind == "v":
                    mm = project_rows(bank, lane.xT, wv_sb, 2 * j)
                elif kind == "kp":
                    t, half = divmod(j, 2)
                    if lane is main and isinstance(i, int) and i == j == 0:
                        pe.wait_ge(low_ready, 1)
                    for b in range(2):
                        for part in range(2):
                            mm = pe.matmul(bank[:, b * (G // 2):(b + 1) * (G // 2)],
                                           lane.k_hl[:, 2 * half + b, t * P:(t + 1) * P],
                                           rw_hl[:, part, 2 * half + b, :], start=(part == 0), stop=(part == 1))
                else:
                    pe.wait_ge(lane.eps, i * T + j + 1)
                    for c in range(FC):
                        mm = pe.matmul(bank[:, c * VW:(c + 1) * VW], lane.kp[:, c * P:(c + 1) * P],
                                       lane.v[:, j % 2, c, :], start=True, stop=True)
                mm.then_inc(lane.full, 1)

            pe.wait_ge(pool_prep, 7)
            fill_lanes(kv_use, prep)
            pe.wait_ge(prep_low, 6)
            pe.wait_ge(low_ready, 3)
            pe.wait_ge(kv2_read, FILL * KV_USES)

            def body(it, par, kv, at, rt, ff, last, batch):
                a, m, s, n = it, it - ATTN_LAG, it - ROUTE_LAG, it - FFN_LAG
                other = 1 - par

                def product(bank, w_hl, wcols, src_hl, scols, swap=False):
                    terms = [(0, 0), (0, 1), (1, 0)]
                    for k in range(KD):
                        for i, (wp, sp) in enumerate(terms):
                            wt, st = w_hl[:, wp, k, wcols], src_hl[:, sp, k, scols]
                            mm = pe.matmul(bank[:], st if swap else wt, wt if swap else st,
                                           start=(k == 0 and i == 0), stop=(k == KD - 1 and i == 2))
                    return mm

                def at_use(kind, j):
                    wait(pe, at_read, m * AT_USES + AT_U[kind, j])
                    if kind == "turn":
                        if j == 0:
                            pe.wait_ge(xb_loaded, (m + 1) * 16)
                        mm = turn(at_bank, xb, j)
                    elif kind == "q":
                        mm = project(at_bank, wq_sb, xbT, j)
                    elif kind == "qp":
                        for part in range(2):
                            mm = pe.matmul(at_bank[:], rw_hl[:, part, j // 2, (j % 2) * P:(j % 2 + 1) * P],
                                           qT_hl[:, j // 2, :], start=(part == 0), stop=(part == 1))
                    elif kind == "qkv":
                        pe.wait_ge(qp_eps, m * FC + 2 * j + 2)
                        if j == 0:
                            pe.wait_ge(blocks_ready, batch)
                        W = 2 * (DK + 1)
                        for t in range(T):
                            for c in range(2):
                                mm = pe.matmul(at_bank[:, (2 * t + c) * W:(2 * t + c + 1) * W],
                                               qp[:, (2 * j + c) % 4, t * P:(t + 1) * P],
                                               kv_blocks[:, 2 * j + c].rearrange("p a b -> p (a b)"),
                                               start=True, stop=True)
                    elif kind == "back":
                        mm = turn(at_bank, x1, j)
                    elif kind == "wo":
                        mm = project_rows(at_bank, attnT, wo_sb, 2 * j)
                    else:
                        pe.wait_ge(x1_ready, (m + 1) * T)
                        mm = turn(at_bank, x1, j)
                    mm.then_inc(at_full, 1)

                def rt_use(t):
                    if t == 0:
                        pe.wait_ge(at_read, (s + 1) * AT_USES)
                    wait(pe, rt_read, s * T + t)
                    product(rt_bank, route_hl, slice(0, G), x1T_hl[:, other], slice(t * P, (t + 1) * P),
                            swap=True).then_inc(rt_full, 1)

                def hidden(bank, w_hl, c):
                    product(bank, w_hl, slice(c * P, (c + 1) * P), x1T_hl[:, par],
                            slice(0, G)).then_inc(ring_full, 1)

                def ff_gate(c):
                    wait(pe, h_ready, n * C + c)
                    hidden(ring[c % 2], wg_hl, c)

                def ff_up(c):
                    wait(pe, ring_act, (n * C + c) * 2)
                    hidden(ring[1 - c % 2], wu_hl, c)

                def ff_dots(c):
                    pe.wait_ge(ring_act, (n * C + c) * 2 + 1)
                    hidden(ring[c % 2], downT_hl, c)

                def ff_weights(c):
                    wait(pe, wexp_ready, n * C + c)
                    if c == 0:
                        pe.wait_ge(prob_ready, (n + 1) * T)
                    for t in range(T):
                        mm = pe.transpose(pt_bank[:, t * P:(t + 1) * P], prob[:, par, t, c * P:(c + 1) * P],
                                          ident)
                    mm.then_inc(pt_full, 1)

                def ff_out(c, pair):
                    if pair == 0:
                        if c == 0:
                            wait(pe, y_read, n * 2)
                        pe.wait_ge(h_ready, n * C + c + 1)
                        pe.wait_ge(wexp_ready, n * C + c + 1)
                    for t in (2 * pair, 2 * pair + 1):
                        rows = y_bank[pair][:, (t % 2) * D:(t % 2 + 1) * D]
                        if c == C - 2:
                            for k in range(KD):
                                for part in range(2):
                                    pe.matmul(rows[:, k * P:(k + 1) * P],
                                              x1T_hl[:, par, part, k, t * P:(t + 1) * P], ident_r[:],
                                              start=False, stop=False, skip_group_check=True)
                        pe.matmul(rows, gate[:, c % 2, t * P:(t + 1) * P], wd_sb[:, c, :],
                                  start=(c == 0 and t % 2 == 0), stop=False, skip_group_check=True)
                        mm = pe.matmul(rows, wexp[:, c % 2, t * P:(t + 1) * P], up_sb[:, c, :],
                                       start=False, stop=(c == C - 1), skip_group_check=True)
                    if pair == 1:
                        mm.then_inc(y_full, 1)

                for c in range(C):
                    if kv:
                        for use in KV_FIRST[c]:
                            kv_use(main, in_main(a), *use)
                    if ff:
                        ff_gate(c)
                    if at:
                        for use in AT_EARLY[c]:
                            at_use(*use)
                    if ff:
                        ff_up(c)
                    if rt and c % 2 == 0:
                        rt_use(c // 2)
                    if kv:
                        for use in KV_EARLY[c]:
                            kv_use(main, in_main(a), *use)
                    if ff:
                        ff_dots(c)
                    if at:
                        for use in AT_MID[c]:
                            at_use(*use)
                    if ff:
                        ff_weights(c)
                        if c:
                            ff_out(c - 1, 0)
                    if kv:
                        for use in KV_LATE[c]:
                            kv_use(main, in_main(a), *use)
                    if ff and c:
                        ff_out(c - 1, 1)
                    if ff and c == C - 1:
                        ff_out(c, 0)
                    if at:
                        for use in AT_LATE[c][:1]:
                            at_use(*use)
                    if ff and c == C - 1:
                        ff_out(c, 1)
                    if at:
                        for use in AT_LATE[c][1:]:
                            at_use(*use)

            schedule(pe, body, lambda b: None)

        @block.scalar
        def _(act):
            banks = ring

            def prep(k):
                bank = banks[k % 2]
                if k < PREP_WG:
                    act.wait_ge(prep_full, k + 1)
                elif k == PREP_WG:
                    act.wait_ge(w_loaded, W_ALL)
                if k < 4:
                    half, quad = divmod(k, 2)
                    act.copy(downT_hl[:, 0, half, quad * G:(quad + 1) * G], bank[:]).then_inc(high_ready, 1)
                elif k < 6:
                    act.copy(wrqT[:, :, (k - 4) * P:(k - 3) * P],
                             bank[:].rearrange("p (b d) -> p b d", b=4)).then_inc(prep_read, 1)
                elif k == 6:
                    act.copy(keysT, bank[:, 0:4 * NK].rearrange("p (b k) -> p b k", k=NK)).then_inc(prep_read, 1)
                elif k < PREP_WG:
                    act.copy(route_half(0, k - 7), bank[:].rearrange("p (b n) -> p b n", n=NK)).then_inc(high_ready, 1)
                elif k == PREP_WG:
                    act.copy(wg_hl[:, 0], wg_rows).then_inc(high_ready, 1)
                else:
                    act.copy(wu_hl[:, 0], wu_rows).then_inc(high_ready, 1)

            def highs(blocks, half, bank, bias, s):
                for i in range(2):
                    rows = slice(i * (P // 2), (i + 1) * (P // 2))
                    act.activation(blocks[rows, 2 * half + i, :], bank[rows], ACT.Identity,
                                   bias=bias[rows, half:half + 1]).then_inc(s, 1)

            def kv_use(lane, i, kind, j):
                if kind in ("v", "sum"):
                    return
                act.wait_ge(lane.full, i * KV_USES + KV_U[kind, j] + 1)
                if kind == "turn":
                    act.copy(lane.xT[:, j, :], lane.bank[:]).then_inc(lane.read, 1)
                elif kind == "k":
                    highs(lane.k_hl, j, lane.bank, bk_sb, lane.high)
                else:
                    act.activation(lane.kp[:, (j % 2) * G:(j % 2 + 1) * G], lane.bank[:],
                                   ACT.Relu).then_inc(lane.read, 1)

            act.wait_ge(rw_loaded, RW_ALL)
            act.copy(rw_hl[:, 0], rw_rows).then_inc(rw_high, 1)
            fill_lanes(kv_use, prep)

            def body(it, par, kv, at, rt, ff, last, batch):
                a, m, s, n = it, it - ATTN_LAG, it - ROUTE_LAG, it - FFN_LAG

                def at_use(kind, j):
                    if kind in ("qkv", "wo"):
                        return
                    act.wait_ge(at_full, m * AT_USES + AT_U[kind, j] + 1)
                    if kind == "turn":
                        act.copy(xbT[:, j, :], at_bank[:]).then_inc(at_read, 1)
                    elif kind == "q":
                        highs(qT_hl, j, at_bank, bq_sb, q_high)
                    elif kind == "qp":
                        act.activation(qp[:, j % 4, :], at_bank[:], ACT.Relu).then_inc(at_read, 1)
                    elif kind == "back":
                        act.copy(attnT[:, j, :], at_bank[:]).then_inc(at_read, 1)
                    else:
                        act.copy(x1T_hl[:, par, 0, j, :], at_bank[:]).then_inc(x1_high, 1)

                def rt_use(t):
                    act.wait_ge(rt_read, s * T + t + 1)
                    act.wait_ge(rt_dve, s * RT_STEPS + t * len(RT_TILE) + RT_AT["less"])
                    act.activation(ex[:], ex[:], ACT.Exp).then_inc(rt_exp, 1)

                def ff_gate(c):
                    act.wait_ge(ring_full, n * (3 * C) + 3 * c + 1)
                    wait(act, y_full, n * C + c - 1)
                    act.activation(gate[:, c % 2], ring[c % 2][:], ACT.Silu,
                                   bias=bg_sb[:, c:c + 1]).then_inc(ring_act, 1)

                def ff_dots(c):
                    act.wait_ge(ring_full, n * (3 * C) + 3 * c + 3)
                    act.activation(wexp[:, c % 2], ring[c % 2][:], ACT.Silu).then_inc(ring_act, 1)

                for c in range(C):
                    if kv:
                        for use in KV_FIRST[c]:
                            kv_use(main, in_main(a), *use)
                    if ff:
                        ff_gate(c)
                    if at:
                        for use in AT_EARLY[c]:
                            at_use(*use)
                    if kv:
                        for use in KV_EARLY[c]:
                            kv_use(main, in_main(a), *use)
                    if ff:
                        ff_dots(c)
                    if at:
                        for use in AT_MID[c]:
                            at_use(*use)
                    if rt and c % 2 == 0 and c:
                        rt_use(c // 2)
                    if kv:
                        for use in KV_LATE[c]:
                            kv_use(main, in_main(a), *use)
                    if at:
                        for use in AT_LATE[c]:
                            at_use(*use)
                    if rt and c == 0:
                        rt_use(0)

            schedule(act, body, lambda b: None)

        @block.vector
        def _(dve):
            dve.memset(kv_sum[:], 0.0).then_inc(sum_cleared, 1)
            banks = ring

            def low(out, whole, high, s):
                dve.tensor_tensor(out, whole, high.bitcast(F32), ALU.subtract).then_inc(s, 1)

            def prep(k):
                bank = banks[k % 2]
                if k < 4:
                    half, quad = divmod(k, 2)
                    cols = slice(quad * G, (quad + 1) * G)
                    dve.wait_ge(high_ready, k + 1)
                    low(downT_hl[:, 1, half, cols], bank[:], downT_hl[:, 0, half, cols], prep_low)
                elif k in (7, 8):
                    dve.wait_ge(high_ready, k - 2)
                    low(route_half(1, k - 7), bank[:].rearrange("p (b n) -> p b n", n=NK),
                        route_half(0, k - 7), prep_low)
                elif k == PREP_WG:
                    dve.wait_ge(w_loaded, W_ALL)
                    dve.wait_ge(high_ready, 7)
                    low(wg_hl[:, 1], wg_rows, wg_hl[:, 0], low_ready)
                elif k == PREP_WU:
                    dve.wait_ge(high_ready, 8)
                    low(wu_hl[:, 1], wu_rows, wu_hl[:, 0], low_ready)

            def lows(blocks, half, bank, bias, high, group, s):
                for i in range(2):
                    dve.wait_ge(high, group * (2 * KD) + 2 * half + i + 1)
                    rows, others = (slice(k * (P // 2), (k + 1) * (P // 2)) for k in (i, 1 - i))
                    ins = dve.scalar_tensor_tensor(out=blocks[others, 2 * half + i, :], in0=bank[rows],
                                                   scalar=bias[rows, half:half + 1],
                                                   in1=blocks[rows, 2 * half + i, :].bitcast(F32),
                                                   op0=ALU.add, op1=ALU.subtract)
                ins.then_inc(s, 1)

            def pair(bank):
                return bank[:].rearrange("p (t d) -> p t d", t=2)

            def kv_use(lane, i, kind, j, batch=0):
                if kind == "k":
                    lows(lane.k_hl, j, lane.bank, bk_sb, lane.high, i, lane.read)
                elif kind == "v":
                    dve.wait_ge(lane.full, i * KV_USES + KV_U[kind, j] + 1)
                    dve.tensor_tensor(lane.v[:, :, :, 0:2 * DK],
                                      lane.bank[:].rearrange("p (t c w) -> p t c w", t=2, c=FC),
                                      bcast(bv_sb[:].rearrange("p (c w) -> p c w", c=FC).unsqueeze(1),
                                            [P, 2, FC, 2 * DK]), ALU.add).then_inc(lane.read, 1)
                elif kind == "sum":
                    dve.wait_ge(lane.full, i * KV_USES + KV_U[kind, j] + 1)
                    dve.wait_ge(sum_cleared, batch + 1)
                    dve.tensor_tensor(kv_sum[:], lane.bank[:, 0:FC * VW].rearrange("p (c w) -> p c w", c=FC),
                                      kv_sum[:], ALU.add).then_inc(lane.read, 1)

            def fill_use(lane, i, kind, j):
                if kind == "sum":
                    if lane is second:
                        dve.wait_ge(kv_read, i * KV_USES + KV_U[kind, j] + 1)
                    elif i or j:
                        before = i * KV_USES + KV_U["sum", j - 1] if j else (i - 1) * KV_USES + KV_U["sum", T - 1]
                        dve.wait_ge(kv2_read, before + 1)
                kv_use(lane, i, kind, j)

            dve.wait_ge(rw_high, 1)
            low(rw_hl[:, 1], rw_rows, rw_hl[:, 0], low_ready)
            dve.wait_ge(pool_prep, 7)
            fill_lanes(fill_use, prep)

            def body(it, par, kv, at, rt, ff, last, batch):
                a, m, s, n, f = it, it - ATTN_LAG, it - ROUTE_LAG, it - FFN_LAG, it - LAST_LAG
                other = 1 - par
                at_steps = Chain(dve, at_dve, m, AT_STEPS)
                rt_steps = Chain(dve, rt_dve, s, RT_STEPS)
                y_steps = Chain(dve, y_dve, f, Y_STEPS)
                marks = {}

                def statistics(rows, stats, mv, steps):
                    for t in range(T):
                        steps.mark(dve.bn_stats(stats[:, t, :], rows[:, t, :]))
                    steps.wait_apart()
                    for t in range(T):
                        steps.mark(dve.bn_aggr(mv[:, t, :], stats[:, t, :]))

                def at_use(kind, j):
                    if kind == "q":
                        lows(qT_hl, j, at_bank, bq_sb, q_high, m, at_read)
                    elif kind == "qkv":
                        heads = at_bank[:, 0:4 * T * (DK + 1)].rearrange("p (t h w) -> p t h w", t=T, h=4)
                        rows = x1[:].rearrange("p t (i h w) -> p t i h w", i=4, h=4)[:, :, j]
                        if j == 0 and last:
                            dve.wait_ge(y_stored, (f + 1) * 16)
                        dve.wait_ge(at_full, m * AT_USES + AT_U[kind, j] + 1)
                        at_steps.mark(dve.tensor_scalar(den[:], heads[:, :, :, DK], ATTN_EPS, None, ALU.add))
                        at_steps.wait()
                        at_steps.mark(dve.reciprocal(den[:], den[:]))
                        at_steps.wait()
                        dve.tensor_tensor(rows, heads[:, :, :, 0:DK],
                                          bcast(den[:].unsqueeze(3), [P, T, 4, DK]),
                                          ALU.mult).then_inc(at_read, 1)
                    elif kind == "wo":
                        if j == 0:
                            dve.wait_ge(xb_bias, m + 1)
                        dve.wait_ge(at_full, m * AT_USES + AT_U[kind, j] + 1)
                        dve.tensor_tensor(x1[:, 2 * j:2 * j + 2, :], pair(at_bank), xb[:, 2 * j:2 * j + 2, :],
                                          ALU.add).then_inc(at_read, 1)
                    elif kind == "next":
                        dve.wait_ge(x1_high, m * 2 + j + 1)
                        low(x1T_hl[:, par, 1, j, :], at_bank[:], x1T_hl[:, par, 0, j, :], at_read)

                def norm1_stats():
                    dve.wait_ge(at_read, m * AT_USES + AT_U["wo", 1] + 1)
                    statistics(x1, stats, mv1, at_steps)

                def norm1():
                    dve.wait_ge(rstd1_ready, m + 1)
                    for t in range(T):
                        dve.tensor_scalar(x1[:, t, :], x1[:, t, :], mv1[:, t, 0:1], rstd1[:, t:t + 1],
                                          ALU.subtract, ALU.mult).then_inc(x1_ready, 1)

                def scores(t):
                    wait_apart(dve, (rt_dve, rt_steps.base + rt_steps.k), (rt_full, s * T + t + 1))
                    for g in range(2 * RH):
                        ins = dve.max(top[:, g, :], rt_bank[:, g * NK:(g + 1) * NK])
                    rt_steps.mark(ins)
                    rt_steps.wait()
                    dve.tensor_tensor(ex[:, :, 0:NK], rt_bank[:].rearrange("p (g k) -> p g k", k=NK),
                                      bcast(top[:, :, 0:1], [P, 2 * RH, NK]), ALU.subtract).then_inc(rt_read, 1)
                    rt_steps.mark(dve.tensor_tensor(ex[:, :, NK:], top[:], bcast(top[:, :, 0:1], [P, 2 * RH, TOP]),
                                                    ALU.subtract))

                def choose(t):
                    dve.wait_ge(rt_exp, s * T + t + 1)
                    rt_steps.mark(dve.tensor_tensor(
                        cand[:], bcast(ex[:, 0:RH, NK:].unsqueeze(3), [P, RH, TOP, TOP]),
                        bcast(ex[:, RH:, NK:].unsqueeze(2), [P, RH, TOP, TOP]), ALU.mult))
                    rt_steps.wait_apart()
                    for h in range(RH):
                        ins = dve.max(best[:, h, :], cand[:, h].rearrange("p a b -> p (a b)"))
                    rt_steps.mark(ins)
                    rt_steps.wait()
                    rt_steps.mark(dve.reduce_sum(zsum[:], best[:], AX.X))
                    rt_steps.wait()
                    marks["rz"] = rt_steps.mark(dve.reciprocal(rz[:], zsum[:]))

                def keep(t, h):
                    dve.wait_ge(spread_ready, s * (RH * T) + t * RH + h + 1)
                    g = grid[:, h % 2].rearrange("p a b -> p (a b)")
                    marks["keep", h] = rt_steps.mark(dve.scalar_tensor_tensor(
                        out=g, in0=g, scalar=best[:, h, TOP - 1:TOP], in1=g, op0=ALU.is_ge, op1=ALU.mult))

                def add_head(t, h):
                    g = grid[:, h % 2].rearrange("p a b -> p (a b)")
                    row = prob[:, other, t, :]
                    rt_steps.wait(marks["keep", h])
                    if h == 0:
                        rt_steps.wait(max(marks["rz"], marks["keep", h]))
                        if t == 0:
                            wait(dve, pt_full, (s - 1) * C)
                        ins = dve.tensor_scalar(row, g, rz[:, 0:1], None, ALU.mult)
                    else:
                        rt_steps.wait(marks["add", h - 1])
                        ins = dve.scalar_tensor_tensor(out=row, in0=g, scalar=rz[:, h:h + 1], in1=row,
                                                       op0=ALU.mult, op1=ALU.add,
                                                       accum_out=mass[:, 0:1] if h == RH - 1 else None)
                    marks["add", h] = rt_steps.mark(ins)

                def clamp(t):
                    rt_steps.wait()
                    rt_steps.mark(dve.tensor_scalar(mass[:, 1:2], mass[:, 0:1], -1.0, float(RH), ALU.mult, ALU.add))
                    rt_steps.wait()
                    last = prob[:, other, t, NEXP - 1:NEXP]
                    dve.tensor_tensor(last, last, mass[:, 1:2], ALU.add).then_inc(prob_ready, 1)

                def ff_h(c):
                    dve.wait_ge(ring_full, n * (3 * C) + 3 * c + 2)
                    dve.wait_ge(ring_act, n * (2 * C) + 2 * c + 1)
                    dve.scalar_tensor_tensor(out=gate[:, c % 2], in0=ring[1 - c % 2][:], scalar=bu_sb[:, c:c + 1],
                                             in1=gate[:, c % 2], op0=ALU.add, op1=ALU.mult).then_inc(h_ready, 1)

                def ff_wexp(c):
                    dve.wait_ge(pt_full, n * C + c + 1)
                    dve.wait_ge(ring_act, n * (2 * C) + 2 * c + 2)
                    dve.tensor_tensor(wexp[:, c % 2], pt_bank[:], wexp[:, c % 2], ALU.mult).then_inc(wexp_ready, 1)

                def y_rows():
                    dve.wait_ge(y_full, (f + 1) * C)
                    dve.wait_ge(at_full, (min(m, NG) if isinstance(m, int) else m) * AT_USES)
                    wait(dve, y_stored, f * 16)
                    for i in range(2):
                        dve.tensor_tensor(y_sb[:, 2 * i:2 * i + 2, :], pair(y_bank[i]),
                                          bcast(bd_sb[:].unsqueeze(1), [P, 2, D]), ALU.add).then_inc(y_read, 1)
                    dve.wait_ge(y_read, (f + 1) * 2)
                    statistics(y_sb, stats, mv2, y_steps)

                def norm2():
                    dve.wait_ge(rstd2_ready, f + 1)
                    for t in range(T):
                        dve.tensor_scalar(y_sb[:, t, :], y_sb[:, t, :], mv2[:, t, 0:1], rstd2[:, t:t + 1],
                                          ALU.subtract, ALU.mult).then_inc(y_ready, 1)

                def uses(kinds):
                    for use in kinds:
                        if use[0] in ("k", "v", "sum") and kv:
                            kv_use(main, in_main(a), *use, batch=batch)
                        if use[0] in ("q", "qkv", "wo", "next") and at:
                            at_use(*use)

                for c in range(C):
                    t, odd = divmod(c, 2)
                    if last and c == 0:
                        y_rows()
                    uses(KV_FIRST[c])
                    if c == 1:
                        uses(AT_EARLY[c])
                    if rt and c == 1:
                        add_head(t, 0)
                    if rt and odd:
                        keep(t, 1)
                    if c != 1:
                        uses(AT_EARLY[c])
                    if ff:
                        ff_h(c)
                    if rt and not odd:
                        scores(t)
                    uses(KV_EARLY[c])
                    if rt and odd:
                        add_head(t, 1)
                    if rt and odd:
                        keep(t, 2)
                    uses(AT_MID[c])
                    if at and c == 6:
                        norm1_stats()
                    if ff:
                        ff_wexp(c)
                    if rt and odd:
                        add_head(t, 2)
                    uses(KV_LATE[c])
                    if at and c == 7:
                        norm1()
                    if rt and odd:
                        keep(t, 3)
                    if rt and not odd and c:
                        choose(t)
                    uses(AT_LATE[c])
                    if last and c == 0:
                        norm2()
                    if rt and c == 0:
                        choose(0)
                    if rt and odd:
                        add_head(t, 3), clamp(t)
                    if rt and not odd:
                        keep(t, 0)
                    if rt and not odd and c:
                        add_head(t, 0)
                assert not rt or rt_steps.k == RT_STEPS
                assert not at or at_steps.k == AT_STEPS

            def batch_end(b):
                dve.wait_ge(kv_read, in_main((b + 1) * BG) * KV_USES)
                if isinstance(b, int) and b == 0:
                    dve.wait_ge(kv2_read, FILL * KV_USES)
                for g2 in range(2):
                    rows = slice(g2 * F, (g2 + 1) * F)
                    dve.tensor_copy(kv_blocks[rows, :, g2, 0:DK], kv_sum[rows, :, g2 * DK:(g2 + 1) * DK])
                    ins = dve.tensor_copy(kv_blocks[rows, :, g2, DK:DK + 1], kv_sum[rows, :, 2 * DK:VW])
                ins.then_inc(blocks_ready, 1)
                dve.wait_ge(blocks_ready, b + 1)
                dve.memset(kv_sum[:], 0.0).then_inc(sum_cleared, 1)

            schedule(dve, body, batch_end)


_INS = ["x", "Wq", "bq", "Wk", "bk", "Wv", "bv", "Wo", "bo", "rw"]
_FFN = ["Wg", "bg", "Wu", "bu", "Wd", "bd", "Wq", "keys", "down_embed", "up_embed"]


def kernel(**inputs):
    import numpy as _np
    import concourse.bacc as _bacc
    from concourse import mybir as _mybir
    from concourse.bass_utils import run_bass_kernel_spmd as _run

    nc = _bacc.Bacc("TRN2", target_bir_lowering=False, num_devices=1)
    arrays, args = {}, []
    for name in [f"L0_attn_{n}" for n in _INS] + [f"L0_ffn_{n}" for n in _FFN]:
        a = _np.ascontiguousarray(inputs[name])
        arrays[f"in_{name}"] = a
        args.append(nc.dram_tensor(f"in_{name}", a.shape, _mybir.dt.from_np(a.dtype), kind="ExternalInput").ap())
    shape = inputs["L0_attn_x"].shape
    args.append(nc.dram_tensor("out_y", shape, _mybir.dt.float32, kind="ExternalOutput").ap())
    block_kernel(nc, *args)
    r = _run(nc, [arrays], core_ids=[0])
    return r.results[0]["out_y"]
```
